# Optimizing a Trainium2 kernel written in Bass

```python
import numpy as np
import jax
import jax.numpy as jnp

def _softmax(x, axis=-1):
    return jax.nn.softmax(x, axis=axis)

def _gelu(x):
    return jax.nn.gelu(x, approximate=True)

def _silu(x):
    return jax.nn.silu(x)

def _sigmoid(x):
    return jax.nn.sigmoid(x)

def _layernorm(x, axis=-1, eps=1e-05):
    m = jnp.mean(x, axis=axis, keepdims=True)
    v = jnp.var(x, axis=axis, keepdims=True)
    return (x - m) / jnp.sqrt(v + eps)

def _scatter_add(tgt, idx, src, axis=0):
    return tgt.at[idx].add(src)

def _segment_sum(src, seg, n):
    return jax.ops.segment_sum(src, seg, n)
kernel_name = 'mk_dlrm_tower_d1_rec_r8_f508f8'

def setup_inputs(seed: int=0):
    np.random.seed(seed)
    _w = jnp.asarray

    def _rec_inputs():
        import jax
        import jax.numpy as jnp
        _tk = jax.random.key(seed)
        ids = jnp.stack([jax.random.randint(jax.random.fold_in(_tk, 200 + f), (512,), 0, v, jnp.int32) for f, v in enumerate([12500, 1000, 12500, 125000, 12500, 12500, 12500, 1000, 12500, 1250, 1000, 12500, 12500, 1000, 1000, 1000, 1250, 1000, 1250, 12500, 1000, 1000, 1250, 1000, 1000, 1000])], axis=1)
        tbl_0 = 0.05 * jax.random.normal(jax.random.fold_in(_tk, 500 + 0), (12500, 128), jnp.float32)
        tbl_1 = 0.05 * jax.random.normal(jax.random.fold_in(_tk, 500 + 1), (1000, 128), jnp.float32)
        tbl_2 = 0.05 * jax.random.normal(jax.random.fold_in(_tk, 500 + 2), (12500, 128), jnp.float32)
        tbl_3 = 0.05 * jax.random.normal(jax.random.fold_in(_tk, 500 + 3), (125000, 128), jnp.float32)
        tbl_4 = 0.05 * jax.random.normal(jax.random.fold_in(_tk, 500 + 4), (12500, 128), jnp.float32)
        tbl_5 = 0.05 * jax.random.normal(jax.random.fold_in(_tk, 500 + 5), (12500, 128), jnp.float32)
        tbl_6 = 0.05 * jax.random.normal(jax.random.fold_in(_tk, 500 + 6), (12500, 128), jnp.float32)
        tbl_7 = 0.05 * jax.random.normal(jax.random.fold_in(_tk, 500 + 7), (1000, 128), jnp.float32)
        tbl_8 = 0.05 * jax.random.normal(jax.random.fold_in(_tk, 500 + 8), (12500, 128), jnp.float32)
        tbl_9 = 0.05 * jax.random.normal(jax.random.fold_in(_tk, 500 + 9), (1250, 128), jnp.float32)
        tbl_10 = 0.05 * jax.random.normal(jax.random.fold_in(_tk, 500 + 10), (1000, 128), jnp.float32)
        tbl_11 = 0.05 * jax.random.normal(jax.random.fold_in(_tk, 500 + 11), (12500, 128), jnp.float32)
        tbl_12 = 0.05 * jax.random.normal(jax.random.fold_in(_tk, 500 + 12), (12500, 128), jnp.float32)
        tbl_13 = 0.05 * jax.random.normal(jax.random.fold_in(_tk, 500 + 13), (1000, 128), jnp.float32)
        tbl_14 = 0.05 * jax.random.normal(jax.random.fold_in(_tk, 500 + 14), (1000, 128), jnp.float32)
        tbl_15 = 0.05 * jax.random.normal(jax.random.fold_in(_tk, 500 + 15), (1000, 128), jnp.float32)
        tbl_16 = 0.05 * jax.random.normal(jax.random.fold_in(_tk, 500 + 16), (1250, 128), jnp.float32)
        tbl_17 = 0.05 * jax.random.normal(jax.random.fold_in(_tk, 500 + 17), (1000, 128), jnp.float32)
        tbl_18 = 0.05 * jax.random.normal(jax.random.fold_in(_tk, 500 + 18), (1250, 128), jnp.float32)
        tbl_19 = 0.05 * jax.random.normal(jax.random.fold_in(_tk, 500 + 19), (12500, 128), jnp.float32)
        tbl_20 = 0.05 * jax.random.normal(jax.random.fold_in(_tk, 500 + 20), (1000, 128), jnp.float32)
        tbl_21 = 0.05 * jax.random.normal(jax.random.fold_in(_tk, 500 + 21), (1000, 128), jnp.float32)
        tbl_22 = 0.05 * jax.random.normal(jax.random.fold_in(_tk, 500 + 22), (1250, 128), jnp.float32)
        tbl_23 = 0.05 * jax.random.normal(jax.random.fold_in(_tk, 500 + 23), (1000, 128), jnp.float32)
        tbl_24 = 0.05 * jax.random.normal(jax.random.fold_in(_tk, 500 + 24), (1000, 128), jnp.float32)
        tbl_25 = 0.05 * jax.random.normal(jax.random.fold_in(_tk, 500 + 25), (1000, 128), jnp.float32)
        _rk = jax.random.fold_in(_tk, 7)
        r_dense_features = -0.000520686 + 1.00062 * jax.random.normal(jax.random.fold_in(_rk, 101), (512, 128), jnp.float32)
        W_top1 = 0.0405887 * jax.random.normal(jax.random.fold_in(_tk, 801), (607, 512), jnp.float32)
        W_top2 = 0.0441942 * jax.random.normal(jax.random.fold_in(_tk, 802), (512, 256), jnp.float32)
        W_top3 = 0.0625 * jax.random.normal(jax.random.fold_in(_tk, 803), (256, 1), jnp.float32)
        b_top1 = jnp.zeros((512,), jnp.float32)
        b_top2 = jnp.zeros((256,), jnp.float32)
        return (r_dense_features, ids, tbl_0, tbl_1, tbl_2, tbl_3, tbl_4, tbl_5, tbl_6, tbl_7, tbl_8, tbl_9, tbl_10, tbl_11, tbl_12, tbl_13, tbl_14, tbl_15, tbl_16, tbl_17, tbl_18, tbl_19, tbl_20, tbl_21, tbl_22, tbl_23, tbl_24, tbl_25, W_top1, b_top1, W_top2, b_top2, W_top3)
    r_dense_features, ids, tbl_0, tbl_1, tbl_2, tbl_3, tbl_4, tbl_5, tbl_6, tbl_7, tbl_8, tbl_9, tbl_10, tbl_11, tbl_12, tbl_13, tbl_14, tbl_15, tbl_16, tbl_17, tbl_18, tbl_19, tbl_20, tbl_21, tbl_22, tbl_23, tbl_24, tbl_25, W_top1, b_top1, W_top2, b_top2, W_top3 = _rec_inputs()

    def _L0_rec_setup():
        import jax, jax.numpy as jnp
        import numpy as np
        NUM_SPARSE = 26
        EMBED_DIM = 128
        BATCH = 2048
        key = jax.random.key(seed)
        k1, k2 = jax.random.split(key)
        dense_features = jax.random.normal(k1, (BATCH, EMBED_DIM), dtype=jnp.float32)
        sparse_features = jax.random.normal(k2, (BATCH, NUM_SPARSE, EMBED_DIM), dtype=jnp.float32)
        return {'dense_features': dense_features, 'sparse_features': sparse_features}
    _L0_rec_all = _L0_rec_setup()
    _L0_rec_in = {k: v for k, v in _L0_rec_all.items() if k in ()}
    del _L0_rec_all
    return {'r_dense_features': r_dense_features, 'ids': ids, 'tbl_0': tbl_0, 'tbl_1': tbl_1, 'tbl_2': tbl_2, 'tbl_3': tbl_3, 'tbl_4': tbl_4, 'tbl_5': tbl_5, 'tbl_6': tbl_6, 'tbl_7': tbl_7, 'tbl_8': tbl_8, 'tbl_9': tbl_9, 'tbl_10': tbl_10, 'tbl_11': tbl_11, 'tbl_12': tbl_12, 'tbl_13': tbl_13, 'tbl_14': tbl_14, 'tbl_15': tbl_15, 'tbl_16': tbl_16, 'tbl_17': tbl_17, 'tbl_18': tbl_18, 'tbl_19': tbl_19, 'tbl_20': tbl_20, 'tbl_21': tbl_21, 'tbl_22': tbl_22, 'tbl_23': tbl_23, 'tbl_24': tbl_24, 'tbl_25': tbl_25, 'W_top1': W_top1, 'b_top1': b_top1, 'W_top2': W_top2, 'b_top2': b_top2, 'W_top3': W_top3}

def reference(r_dense_features, ids, tbl_0, tbl_1, tbl_2, tbl_3, tbl_4, tbl_5, tbl_6, tbl_7, tbl_8, tbl_9, tbl_10, tbl_11, tbl_12, tbl_13, tbl_14, tbl_15, tbl_16, tbl_17, tbl_18, tbl_19, tbl_20, tbl_21, tbl_22, tbl_23, tbl_24, tbl_25, W_top1, b_top1, W_top2, b_top2, W_top3):
    import jax
    import jax.numpy as jnp

    def _L0_rec_ref(dense_features, sparse_features):
        import jax, jax.numpy as jnp
        import numpy as np
        NUM_SPARSE = 26
        EMBED_DIM = 128
        BATCH = 2048
        F = NUM_SPARSE + 1
        combined = jnp.concatenate([dense_features[:, None, :], sparse_features], axis=1)
        interactions = jnp.einsum('bfd,bgd->bfg', combined, combined)
        iu, ju = jnp.triu_indices(F, k=1)
        interactions_flat = interactions[:, iu, ju]
        return jnp.concatenate([dense_features, interactions_flat], axis=1)
    e = jnp.stack([tbl_0[ids[:, 0]], tbl_1[ids[:, 1]], tbl_2[ids[:, 2]], tbl_3[ids[:, 3]], tbl_4[ids[:, 4]], tbl_5[ids[:, 5]], tbl_6[ids[:, 6]], tbl_7[ids[:, 7]], tbl_8[ids[:, 8]], tbl_9[ids[:, 9]], tbl_10[ids[:, 10]], tbl_11[ids[:, 11]], tbl_12[ids[:, 12]], tbl_13[ids[:, 13]], tbl_14[ids[:, 14]], tbl_15[ids[:, 15]], tbl_16[ids[:, 16]], tbl_17[ids[:, 17]], tbl_18[ids[:, 18]], tbl_19[ids[:, 19]], tbl_20[ids[:, 20]], tbl_21[ids[:, 21]], tbl_22[ids[:, 22]], tbl_23[ids[:, 23]], tbl_24[ids[:, 24]], tbl_25[ids[:, 25]]], axis=1)
    z = _L0_rec_ref(r_dense_features, e)
    z = z.reshape(z.shape[0], -1)
    h = jnp.concatenate([z, r_dense_features], axis=1)
    h = jnp.maximum(h @ W_top1 + b_top1, 0.0)
    h = jnp.maximum(h @ W_top2 + b_top2, 0.0)
    y = h @ W_top3
    return y

_drawn_inputs = setup_inputs


def setup_inputs(seed=0):
    import zlib

    import numpy as np

    out = dict(_drawn_inputs(seed))
    spreads = {'b_top1': (0.0, 0.1), 'b_top2': (0.0, 0.1)}
    factors = {}
    for name, (base, spread) in spreads.items():
        noise = np.random.default_rng([zlib.crc32(name.encode()), seed]).standard_normal(out[name].shape)
        drawn = base * np.exp(spread * noise) if base else spread * noise
        out[name] = jnp.asarray(drawn.astype(out[name].dtype))
    for name, factor in factors.items():
        out[name] = (out[name] * factor).astype(out[name].dtype)
    return out
```

```python
import concourse.bass as bass
from concourse import mybir
from contextlib import ExitStack

P = 128
BATCH = 512
TILES = BATCH // P
DIM = 128
TABLES = 26
FEATURES = TABLES + 1
H1, H2 = 512, 256
ROWS = [12500, 1000, 12500, 125000, 12500, 12500, 12500, 1000, 12500, 1250, 1000, 12500, 12500,
        1000, 1000, 1000, 1250, 1000, 1250, 12500, 1000, 1000, 1250, 1000, 1000, 1000]

ONEHOT = [14, 15, 20, 21, 22, 23, 24, 25]
OH_PARTS = 125
OH_PARTS_MAIN = 112
KEPT_RUNS = [(15, 2, 0), (21, 6, 2)]
MAX_CHUNKS = 10
PIECE = MAX_CHUNKS // 2
RAW_SLOTS = 2
PIECE_SLOTS = 2
OH_SLOTS = 3

GROUPS = [[17, 18, 19, 20], [11, 12, 13, 14], [7, 8, 9, 10], [3, 4, 5, 6], [0, 1, 2]]
GPT = len(GROUPS)
GATHER_SLOTS = 3

SPG = 4
QUAD = 32
MOVING = FEATURES + 1
HALF_GROUPS = P // SPG // 2
GSTRIDE = 128
KT = (FEATURES + 3) // 4
ET_SLOTS = TILES - 1
NK = [(FEATURES - q + 3) // 4 for q in range(4)]
BIAS_ROW = 3 * QUAD + 26


def chunks(i):
    return ROWS[ONEHOT[i]] // OH_PARTS


def pair_row(g):
    return DIM + g * TABLES - g * (g - 1) // 2


def build(nc, dense, ids, tables, w1, b1, w2, b2, w3, out):
    fp32, f32r, i32 = mybir.dt.float32, mybir.dt.float32r, mybir.dt.int32
    ALU, ACT = mybir.AluOpType, mybir.ActivationFunctionType
    NOH = len(ONEHOT)
    PIECES = 2 * NOH
    NGROUPS = GPT * TILES
    first_chunk = [sum(chunks(j) for j in range(i)) for i in range(NOH + 1)]

    ctx = ExitStack()
    with ctx:
        def sb(name, shape, dt=fp32):
            return ctx.enter_context(nc.sbuf_tensor(name, shape, dt))

        def ps(name, shape, dt=fp32):
            return ctx.enter_context(nc.psum_tensor(name, shape, dt))

        def sem(name):
            return ctx.enter_context(nc.semaphore(name))

        ident = sb("ident", [P, P])
        ids_i = sb("ids_i", [P, TILES, TABLES], i32)
        ids_f = sb("ids_f", [P, TILES, TABLES])
        ids_bc = sb("ids_bc", [P, 2, BATCH])
        rowid = {c: sb(f"rowid{c}", [P, c]) for c in sorted({chunks(i) for i in range(NOH)})}
        dense_sb = sb("dense_sb", [P, TILES, DIM])
        gathered = sb("gathered", [P, GATHER_SLOTS, 4, DIM])
        et_hi = sb("et_hi", [P, ET_SLOTS, P * QUAD], f32r)
        et_lo = sb("et_lo", [P, ET_SLOTS, P * QUAD], f32r)
        keep_hi = sb("keep_hi", [P, NOH, P], f32r)
        keep_lo = sb("keep_lo", [P, NOH, P], f32r)
        tab_raw = sb("tab_raw", [P, RAW_SLOTS, PIECE * DIM])
        tab_hi = sb("tab_hi", [P, PIECE_SLOTS, PIECE * DIM], f32r)
        tab_lo = sb("tab_lo", [P, PIECE_SLOTS, PIECE * DIM], f32r)
        onehot = sb("onehot", [P, OH_SLOTS, BATCH], f32r)
        w_raw = sb("w_raw", [P, 2, H1])
        w1_hi = sb("w1_hi", [P, KT + 1, H1], f32r)
        w1_lo = sb("w1_lo", [P, KT + 1, H1], f32r)
        w2_hi = sb("w2_hi", [P, H1 // P, H2], f32r)
        w2_lo = sb("w2_lo", [P, H1 // P, H2], f32r)
        w3_bc = sb("w3_bc", [P, H2])
        b2_row = sb("b2_row", [1, H2])
        ones_row = sb("ones_row", [1, P])
        g_raw = sb("g_raw", [P, KT, P])
        g_hi = sb("g_hi", [P, KT, P], f32r)
        g_lo = sb("g_lo", [P, KT, P], f32r)
        h1_sb = sb("h1_sb", [P, H1])
        h1t_hi = sb("h1t_hi", [P, H1 // P, P], f32r)
        h1t_lo = sb("h1t_lo", [P, H1 // P, P], f32r)
        h2w3 = sb("h2w3", [P, H2])
        y = sb("y", [P, TILES])

        gram_ps = ps("gram_ps", [P, 4 * 512])
        trans_ps = ps("trans_ps", [P, 2, 512])
        mlp_ps = ps("mlp_ps", [P, H1])
        misc_ps = ps("misc_ps", [P, 512])

        ids_in = sem("ids_in")
        dense_in = sem("dense_in")
        tab_in = [sem(f"tab_in{s}") for s in range(RAW_SLOTS)]
        w_in = [sem(f"w_in{s}") for s in range(2)]
        small_in = sem("small_in")
        gather_in = [sem(f"gather_in{s}") for s in range(GATHER_SLOTS)]
        ident_zero = sem("ident_zero")
        pool_consts = sem("pool_consts")
        dve_consts = sem("dve_consts")
        ids_f_ready = sem("ids_f_ready")
        ids_ps_ready = sem("ids_ps_ready")
        ids_bc_ready = sem("ids_bc_ready")
        tab_hi_ready = sem("tab_hi_ready")
        tab_lo_ready = sem("tab_lo_ready")
        onehot_ready = sem("onehot_ready")
        chunk_done = sem("chunk_done")
        oh_done = sem("oh_done")
        oh_copied = sem("oh_copied")
        kept_hi_back = sem("kept_hi_back")
        kept_lo_back = sem("kept_lo_back")
        w_sum_ready = sem("w_sum_ready")
        w_hi_ready = sem("w_hi_ready")
        w_lo_ready = sem("w_lo_ready")
        trans_ready = sem("trans_ready")
        trans_hi_done = sem("trans_hi_done")
        trans_lo_done = sem("trans_lo_done")
        gram_ready = sem("gram_ready")
        moved_act = sem("moved_act")
        moved_dve = sem("moved_dve")
        g_hi_ready = sem("g_hi_ready")
        g_lo_ready = sem("g_lo_ready")
        h1_ready = sem("h1_ready")
        h1_relu = sem("h1_relu")
        h1t_ready = sem("h1t_ready")
        h1t_hi_ready = sem("h1t_hi_ready")
        h1t_lo_ready = sem("h1t_lo_ready")
        h2_ready = sem("h2_ready")
        y_ready = sem("y_ready")
        y_out = sem("y_out")

        def f32(ap):
            return ap.bitcast(fp32)

        def et_cols(et, t, f0, n):
            return et[:, t % ET_SLOTS, :].rearrange("p (n f) -> p f n", f=QUAD)[:, f0:f0 + n, :]

        def et_feature(et, f):
            return et[:, :, :].rearrange("p t (n f) -> p t n f", f=QUAD)[:, :, :, f]

        def et_stationary(et, t, j):
            return et[:, t % ET_SLOTS, j * P:(j + 1) * P]

        def et_moving(et, t, j):
            return et_stationary(et, t, j).rearrange("p (s f) -> p s f", f=QUAD)[:, :, 0:MOVING]

        def et_dense(et, t):
            return et[:, t % ET_SLOTS, :].rearrange("p (n f) -> p n f", f=QUAD)[:, :, 0]

        def gram_block(s, q, nk):
            v = gram_ps[QUAD * s:QUAD * s + FEATURES, :].rearrange("p (j c) -> p c j", c=GSTRIDE)
            c0 = s * MOVING + q
            return v[:, c0:c0 + 4 * (nk - 1) + 1:4, :]

        def g_block(s, q, nk, h):
            v = g_raw[QUAD * q:QUAD * q + FEATURES, 0:nk, :].rearrange("p k (j s) -> p k s j", s=SPG)
            return v[:, :, s, h * HALF_GROUPS:(h + 1) * HALF_GROUPS]

        w_stages = [(k, n % 2) for n, k in enumerate(range(KT - 1, -1, -1))]
        N_PAIR = len(w_stages)
        STAGE_DENSE, STAGE_W2 = N_PAIR, N_PAIR + 1
        w_count = [0, 0]
        w_need = []
        w_dmas = []
        for k, slot in w_stages:
            dmas = []
            for q in range(4):
                g = 4 * k + q
                n = FEATURES - 1 - g
                if n > 0:
                    dmas.append((w_raw[QUAD * q + g + 1:QUAD * q + FEATURES, slot, :],
                                 w1[pair_row(g):pair_row(g) + n, :], slot))
            if k == KT - 1:
                dmas.append((w_raw[BIAS_ROW:BIAS_ROW + 1, slot, :], b1.rearrange("(a n) -> a n", a=1), slot))
            w_dmas.append(dmas)
        dense_rows2 = DIM + FEATURES * TABLES // 2
        w_dmas.append([(w_raw[:, 0, :], w1[0:DIM, :], 0),
                       (w_raw[:, 1, :], w1[dense_rows2:dense_rows2 + DIM, :], 1)])
        w2_raw = w_raw[:, :, :].rearrange("p a n -> p (a n)").rearrange("p (c n) -> p c n", n=H2)
        w_dmas.append([(w2_raw[:, 0:2, :], w2.rearrange("(c p) n -> p c n", p=P)[:, 0:2, :], 0),
                       (w2_raw[:, 2:4, :], w2.rearrange("(c p) n -> p c n", p=P)[:, 2:4, :], 1)])
        for dmas in w_dmas:
            for _, _, slot in dmas:
                w_count[slot] += 16
            w_need.append(tuple(w_count))
        NSTAGES = len(w_dmas)

        def stage_after(i):
            return list(range(NSTAGES * i // NOH, NSTAGES * (i + 1) // NOH))

        block = ctx.enter_context(nc.Block())

        @block.sync
        def _(sp):
            sp.dma_start(ids_i[:, :, :], ids.rearrange("(p t) s -> p t s", t=TILES)).then_inc(ids_in, 16)

            def load_piece(n):
                i, h = n // 2, n % 2
                c = chunks(i) // 2
                if n >= RAW_SLOTS:
                    sp.wait_ge(tab_lo_ready, n - RAW_SLOTS + 1)
                src = tables[ONEHOT[i]].rearrange("(p c) d -> p (c d)", p=OH_PARTS)
                src = src[:, h * c * DIM:(h + 1) * c * DIM]
                for a, b in ((0, OH_PARTS_MAIN), (OH_PARTS_MAIN, OH_PARTS)):
                    sp.dma_start(tab_raw[a:b, n % RAW_SLOTS, 0:c * DIM], src[a:b, :])\
                      .then_inc(tab_in[n % RAW_SLOTS], 16)

            def load_stage(w):
                if w == 0:
                    sp.wait_ge(dve_consts, 1)
                elif w >= 2:
                    sp.wait_ge(w_lo_ready, w - 1 if w < N_PAIR else w)
                for dst, src, slot in w_dmas[w]:
                    sp.dma_start(dst, src).then_inc(w_in[slot], 16)

            load_piece(0)
            load_piece(1)
            sp.dma_start(dense_sb[:, :, :], dense.rearrange("(p t) d -> p t d", t=TILES)).then_inc(dense_in, 16)
            sp.dma_start(w3_bc[:, :], w3.rearrange("a b -> (a b)").partition_broadcast(P)).then_inc(small_in, 16)
            sp.dma_start(b2_row[:, :], b2.rearrange("(a n) -> a n", a=1)).then_inc(small_in, 16)
            for i in range(NOH):
                for w in stage_after(i):
                    load_stage(w)
                for n in (2 * i + 2, 2 * i + 3):
                    if n < PIECES:
                        load_piece(n)
            sp.wait_ge(y_ready, TILES)
            sp.dma_start(out.rearrange("(p t) a -> p (t a)", t=TILES), y[:, :]).then_inc(y_out, 16)
            sp.wait_ge(y_out, 16)

        @block.gpsimd
        def _(pool):
            pool.memset(ident[:, :], 0.0).then_inc(ident_zero, 1)
            pool.memset(g_raw[:, KT - 1, :], 0.0).then_inc(ident_zero, 1)
            for c, r in rowid.items():
                pool.iota(r[:, :], pattern=[[1, c]], base=0, channel_multiplier=c,
                          allow_small_or_imprecise_dtypes=True).then_inc(pool_consts, 1)
            pool.wait_ge(ident_zero, 2)
            pool.affine_select(out=ident[:, :], in_=ident[:, :], compare_op=ALU.not_equal, fill=1.0, base=0,
                               pattern=[[-1, P]], channel_multiplier=1).then_inc(pool_consts, 1)
            pool.affine_select(out=g_raw[:, KT - 1, :], in_=g_raw[:, KT - 1, :], compare_op=ALU.not_equal,
                               fill=1.0, base=-BIAS_ROW, pattern=[[0, P]], channel_multiplier=1)\
                .then_inc(pool_consts, 1)
            pool.wait_ge(ids_in, 16)
            for n in range(NGROUPS):
                t, fs = n // GPT, GROUPS[n % GPT]
                if n >= GATHER_SLOTS:
                    pool.wait_ge(trans_ready, n - GATHER_SLOTS + 1)
                for f in fs:
                    if f > 0:
                        pool.indirect_dma_start(
                            out=gathered[:, n % GATHER_SLOTS, f - fs[0], :], out_offset=None, in_=tables[f - 1],
                            in_offset=bass.IndirectOffsetOnAxis(ap=ids_i[:, t, f - 1:f], axis=0),
                        ).then_inc(gather_in[n % GATHER_SLOTS], 16)

        CONSTS = len(rowid) + 2

        gather_need, gather_count = [], [0] * GATHER_SLOTS
        for n in range(NGROUPS):
            gather_count[n % GATHER_SLOTS] += 16 * sum(f > 0 for f in GROUPS[n % GPT])
            gather_need.append(gather_count[n % GATHER_SLOTS])

        order = []
        for i in range(NOH):
            order.append(("table", i))
            order.append(("group", i))
            order += [("weights", w) for w in stage_after(i)]
        done = NOH
        order += [("gram", 0, 0), ("group", 8), ("gram", 0, 1), ("group", 9), ("kept",), ("mlp1", 0),
                  ("gram", 1, 0), ("mlp2", 0), ("group", 10), ("gram", 1, 1), ("mlp1", 1),
                  ("group", 11), ("mlp2", 1), ("group", 12), ("group", 13), ("group", 14),
                  ("gram", 2, 0), ("gram", 2, 1), ("group", 15), ("mlp1", 2), ("group", 16), ("mlp2", 2),
                  ("group", 17), ("group", 18), ("group", 19), ("gram", 3, 0), ("gram", 3, 1),
                  ("mlp1", 3), ("mlp2", 3)]

        @block.tensor
        def _(pe):
            def broadcast_ids(i):
                if i == 0:
                    pe.wait_ge(ids_f_ready, 1)
                    pe.wait_ge(pool_consts, CONSTS)
                else:
                    pe.wait_ge(ids_bc_ready, i)
                for t in range(TILES):
                    s = ONEHOT[i]
                    last = nc.tensor.transpose(misc_ps[:, t * P:(t + 1) * P],
                                               ids_f[:, t, s:s + 1].broadcast_to([P, P]), ident[:, :])
                last.then_inc(ids_ps_ready, 1)

            def table(i):
                if i == 0:
                    broadcast_ids(0)
                if i + 1 < NOH:
                    broadcast_ids(i + 1)
                hi_ps = gram_ps[:, (i % 2) * 1024:(i % 2) * 1024 + 512]
                lo_ps = gram_ps[:, (i % 2) * 1024 + 512:(i % 2) * 1024 + 1024]
                if i >= 2:
                    pe.wait_ge(oh_copied, i - 1)
                C = chunks(i)
                for c in range(C):
                    piece = 2 * i + c // (C // 2)
                    if c % (C // 2) == 0:
                        pe.wait_ge(tab_lo_ready, piece + 1)
                    x = first_chunk[i] + c
                    pe.wait_ge(onehot_ready, x + 1)
                    cc = c % (C // 2)
                    for src, dst in ((tab_hi, hi_ps), (tab_lo, lo_ps)):
                        last = nc.tensor.matmul(dst, src[0:OH_PARTS, piece % PIECE_SLOTS, cc * DIM:(cc + 1) * DIM],
                                                onehot[0:OH_PARTS, x % OH_SLOTS, :],
                                                start=(c == 0), stop=(c == C - 1))
                    last.then_inc(chunk_done, 1)

            def group(n):
                t, fs = n // GPT, GROUPS[n % GPT]
                if n == 0:
                    pe.wait_ge(dense_in, 16)
                if n >= 2:
                    pe.wait_ge(trans_lo_done, n - 1)
                pe.wait_ge(gather_in[n % GATHER_SLOTS], gather_need[n])
                for a, f in enumerate(fs):
                    src = gathered[:, n % GATHER_SLOTS, a, :] if f > 0 else dense_sb[:, t, :]
                    last = nc.tensor.transpose(trans_ps[:, n % 2, a * P:(a + 1) * P], src, ident[:, :])
                last.then_inc(trans_ready, 1)

            def gram(t, h):
                if (t, h) == (0, 0):
                    pe.wait_ge(oh_copied, NOH)
                    pe.wait_ge(dve_consts, 2)
                else:
                    pe.wait_ge(moved_act, 2 * t + h)
                    pe.wait_ge(moved_dve, 2 * t + h)
                if h == 0:
                    pe.wait_ge(trans_lo_done, GPT * (t + 1))
                if t == TILES - 1 and h == 0:
                    pe.wait_ge(kept_hi_back, 1)
                    pe.wait_ge(kept_lo_back, 1)
                for jj in range(HALF_GROUPS):
                    j = h * HALF_GROUPS + jj
                    dst = gram_ps[:, jj * GSTRIDE:jj * GSTRIDE + SPG * MOVING].rearrange("p (s f) -> p s f", f=MOVING)
                    nc.tensor.matmul(dst, et_stationary(et_hi, t, j), et_moving(et_hi, t, j), start=True, stop=False)
                    nc.tensor.matmul(dst, et_stationary(et_hi, t, j), et_moving(et_lo, t, j), start=False, stop=False)
                    last = nc.tensor.matmul(dst, et_stationary(et_lo, t, j), et_moving(et_hi, t, j),
                                            start=False, stop=True)
                last.then_inc(gram_ready, 1)

            def mlp1(t):
                if t == 0:
                    pe.wait_ge(w_lo_ready, NSTAGES)
                else:
                    pe.wait_ge(y_ready, t)
                parts = [(et_dense(et_hi, t), et_dense(et_lo, t), KT)]
                parts += [(g_hi[:, k, :], g_lo[:, k, :], k) for k in range(KT)]
                for n, (hi, lo, k) in enumerate(parts):
                    if n == 1:
                        pe.wait_ge(g_lo_ready, t + 1)
                    nc.tensor.matmul(mlp_ps[:, :], hi, w1_hi[:, k, :], start=(n == 0), stop=False)
                    nc.tensor.matmul(mlp_ps[:, :], hi, w1_lo[:, k, :], start=False, stop=False)
                    last = nc.tensor.matmul(mlp_ps[:, :], lo, w1_hi[:, k, :], start=False, stop=(n == KT))
                last.then_inc(h1_ready, 1)

            def mlp2(t):
                if t == 0:
                    pe.wait_ge(ids_bc_ready, NOH)
                    pe.wait_ge(small_in, 32)
                else:
                    pe.wait_ge(h1t_lo_ready, t)
                pe.wait_ge(h1_relu, t + 1)
                for c in range(H1 // P):
                    last = nc.tensor.transpose(misc_ps[:, c * P:(c + 1) * P], h1_sb[:, c * P:(c + 1) * P], ident[:, :])
                last.then_inc(h1t_ready, 1)
                h2_ps = mlp_ps[:, 0:H2]
                nc.tensor.matmul(h2_ps, ones_row[:, :], b2_row[:, :], start=True, stop=False)
                pe.wait_ge(h1t_lo_ready, t + 1)
                for c in range(H1 // P):
                    nc.tensor.matmul(h2_ps, h1t_hi[:, c, :], w2_hi[:, c, :], start=False, stop=False)
                    nc.tensor.matmul(h2_ps, h1t_hi[:, c, :], w2_lo[:, c, :], start=False, stop=False)
                    last = nc.tensor.matmul(h2_ps, h1t_lo[:, c, :], w2_hi[:, c, :], start=False,
                                            stop=(c == H1 // P - 1))
                last.then_inc(h2_ready, 1)

            steps = {"table": table, "group": group, "gram": gram, "mlp1": mlp1, "mlp2": mlp2}
            for kind, *at in order:
                if kind in steps:
                    steps[kind](*at)

        @block.scalar
        def _(act):
            def broadcast_ids(i):
                act.wait_ge(ids_ps_ready, i + 1)
                if i >= 2:
                    act.wait_ge(onehot_ready, first_chunk[i - 1])
                nc.scalar.activation(ids_bc[:, i % 2, :], misc_ps[:, :], ACT.Copy).then_inc(ids_bc_ready, 1)

            def split_piece(n):
                c = chunks(n // 2) // 2
                act.wait_ge(tab_in[n % RAW_SLOTS], 32 * (n // RAW_SLOTS + 1))
                if n >= PIECE_SLOTS:
                    m = n - PIECE_SLOTS
                    act.wait_ge(chunk_done, first_chunk[m // 2] + (m % 2 + 1) * chunks(m // 2) // 2)
                nc.scalar.activation(tab_hi[0:OH_PARTS, n % PIECE_SLOTS, 0:c * DIM],
                                     tab_raw[0:OH_PARTS, n % RAW_SLOTS, 0:c * DIM], ACT.Copy)\
                  .then_inc(tab_hi_ready, 1)

            def copy_onehot(i):
                f = ONEHOT[i] + 1
                act.wait_ge(chunk_done, first_chunk[i + 1])
                for n, (et, keep) in enumerate(((et_hi, keep_hi), (et_lo, keep_lo))):
                    bank = gram_ps[:, (i % 2) * 1024 + n * 512:(i % 2) * 1024 + (n + 1) * 512]
                    nc.scalar.activation(et_feature(et, f),
                                         bank[:, 0:ET_SLOTS * P].rearrange("p (t n) -> p t n", n=P), ACT.Copy)
                    last = nc.scalar.activation(keep[:, i, :], bank[:, ET_SLOTS * P:], ACT.Copy)
                last.then_inc(oh_copied, 1)

            def table(i):
                if i == 0:
                    broadcast_ids(0)
                    split_piece(0)
                    split_piece(1)
                if i + 1 < NOH:
                    broadcast_ids(i + 1)
                    split_piece(2 * i + 2)
                    split_piece(2 * i + 3)
                copy_onehot(i)

            def group(n):
                t, fs = n // GPT, GROUPS[n % GPT]
                act.wait_ge(trans_ready, n + 1)
                nc.scalar.activation(et_cols(et_hi, t, fs[0], len(fs)),
                                     trans_ps[:, n % 2, 0:len(fs) * P].rearrange("p (f n) -> p f n", n=P), ACT.Copy)\
                  .then_inc(trans_hi_done, 1)

            def weights(w):
                for slot in range(2):
                    act.wait_ge(w_in[slot], w_need[w][slot]) if w_need[w][slot] else None
                if w < N_PAIR:
                    k, slot = w_stages[w]
                    src, dst = w_raw[:, slot, :], w1_hi[:, k, :]
                elif w == STAGE_DENSE:
                    act.wait_ge(w_sum_ready, 1)
                    src, dst = w_raw[:, 0, :], w1_hi[:, KT, :]
                else:
                    src, dst = w2_raw, w2_hi[:, :, :]
                nc.scalar.activation(dst, src, ACT.Copy).then_inc(w_hi_ready, 1)

            def gram(t, h):
                act.wait_ge(gram_ready, 2 * t + h + 1)
                if t == 0 and h == 0:
                    act.wait_ge(dve_consts, 3)
                elif h == 0:
                    act.wait_ge(g_lo_ready, t)
                for s in (0, 1):
                    for q in range(4):
                        last = nc.scalar.activation(g_block(s, q, NK[q], h), gram_block(s, q, NK[q]), ACT.Copy)
                last.then_inc(moved_act, 1)
                if h == 1:
                    act.wait_ge(pool_consts, CONSTS)
                    act.wait_ge(moved_act, 2 * t + 2)
                    act.wait_ge(moved_dve, 2 * t + 2)
                    if t > 0:
                        act.wait_ge(h1_ready, t)
                    nc.scalar.activation(g_hi[:, :, :], g_raw[:, :, :], ACT.Copy).then_inc(g_hi_ready, 1)

            def mlp1(t):
                act.wait_ge(h1_ready, t + 1)
                if t > 0:
                    act.wait_ge(h1t_ready, t)
                nc.scalar.activation(h1_sb[:, :], mlp_ps[:, :], ACT.Relu).then_inc(h1_relu, 1)

            def mlp2(t):
                act.wait_ge(h1t_ready, t + 1)
                if t > 0:
                    act.wait_ge(h2_ready, t)
                nc.scalar.activation(h1t_hi[:, :, :], misc_ps[:, :].rearrange("p (c n) -> p c n", n=P), ACT.Copy)\
                  .then_inc(h1t_hi_ready, 1)

            def kept():
                act.wait_ge(gram_ready, 2)
                for f0, n, i0 in KEPT_RUNS:
                    last = nc.scalar.activation(et_cols(et_hi, TILES - 1, f0, n), f32(keep_hi[:, i0:i0 + n, :]),
                                                ACT.Copy)
                last.then_inc(kept_hi_back, 1)

            steps = {"table": table, "group": group, "weights": weights, "gram": gram, "mlp1": mlp1, "mlp2": mlp2,
                     "kept": kept}
            for kind, *at in order:
                steps[kind](*at)

        @block.vector
        def _(dve):
            def split_piece(n):
                c = chunks(n // 2) // 2
                dve.wait_ge(tab_hi_ready, n + 1)
                nc.vector.tensor_tensor(tab_lo[0:OH_PARTS, n % PIECE_SLOTS, 0:c * DIM],
                                        tab_raw[0:OH_PARTS, n % RAW_SLOTS, 0:c * DIM],
                                        f32(tab_hi[0:OH_PARTS, n % PIECE_SLOTS, 0:c * DIM]), ALU.subtract)\
                  .then_inc(tab_lo_ready, 1)

            def onehots(i, h):
                C = chunks(i)
                for c in range(h * C // 2, (h + 1) * C // 2):
                    x = first_chunk[i] + c
                    if x >= OH_SLOTS:
                        dve.wait_ge(chunk_done, x - OH_SLOTS + 1)
                    nc.vector.tensor_scalar(onehot[0:OH_PARTS, x % OH_SLOTS, :], ids_bc[0:OH_PARTS, i % 2, :],
                                            rowid[C][0:OH_PARTS, c:c + 1], None, ALU.is_equal)\
                      .then_inc(onehot_ready, 1)

            def table(i):
                if i == 0:
                    dve.wait_ge(pool_consts, CONSTS)
                    split_piece(0)
                    split_piece(1)
                dve.wait_ge(ids_bc_ready, i + 1)
                onehots(i, 0)
                onehots(i, 1)
                if i + 1 < NOH:
                    split_piece(2 * i + 2)
                    split_piece(2 * i + 3)

            def group(n):
                t, fs = n // GPT, GROUPS[n % GPT]
                dve.wait_ge(trans_hi_done, n + 1)
                nc.vector.tensor_tensor(et_cols(et_lo, t, fs[0], len(fs)),
                                        trans_ps[:, n % 2, 0:len(fs) * P].rearrange("p (f n) -> p f n", n=P),
                                        f32(et_cols(et_hi, t, fs[0], len(fs))), ALU.subtract)\
                  .then_inc(trans_lo_done, 1)

            def weights(w):
                if w == STAGE_DENSE:
                    for slot in range(2):
                        dve.wait_ge(w_in[slot], w_need[w][slot])
                    nc.vector.tensor_tensor(w_raw[:, 0, :], w_raw[:, 0, :], w_raw[:, 1, :], ALU.add)\
                      .then_inc(w_sum_ready, 1)
                dve.wait_ge(w_hi_ready, w + 1)
                if w < N_PAIR:
                    k, slot = w_stages[w]
                    src, hi, lo = w_raw[:, slot, :], w1_hi[:, k, :], w1_lo[:, k, :]
                elif w == STAGE_DENSE:
                    src, hi, lo = w_raw[:, 0, :], w1_hi[:, KT, :], w1_lo[:, KT, :]
                else:
                    src, hi, lo = w2_raw, w2_hi[:, :, :], w2_lo[:, :, :]
                nc.vector.tensor_tensor(lo, src, f32(hi), ALU.subtract).then_inc(w_lo_ready, 1)

            def gram(t, h):
                dve.wait_ge(gram_ready, 2 * t + h + 1)
                if t > 0 and h == 0:
                    dve.wait_ge(g_hi_ready, t)
                for s in (2, 3):
                    for q in range(4):
                        last = nc.vector.tensor_copy(g_block(s, q, NK[q], h), gram_block(s, q, NK[q]))
                last.then_inc(moved_dve, 1)
                if h == 1:
                    dve.wait_ge(moved_dve, 2 * t + 2)
                    dve.wait_ge(g_hi_ready, t + 1)
                    nc.vector.tensor_tensor(g_lo[:, :, :], g_raw[:, :, :], f32(g_hi[:, :, :]), ALU.subtract)\
                      .then_inc(g_lo_ready, 1)

            def mlp2(t):
                dve.wait_ge(h1t_hi_ready, t + 1)
                nc.vector.tensor_tensor(h1t_lo[:, :, :], misc_ps[:, :].rearrange("p (c n) -> p c n", n=P),
                                        f32(h1t_hi[:, :, :]), ALU.subtract).then_inc(h1t_lo_ready, 1)
                dve.wait_ge(h2_ready, t + 1)
                if t == 0:
                    dve.wait_ge(small_in, 32)
                nc.vector.scalar_tensor_tensor(out=h2w3[:, :], in0=mlp_ps[:, 0:H2], scalar=0.0, in1=w3_bc[:, :],
                                               op0=ALU.max, op1=ALU.mult, accum_out=y[:, t:t + 1])\
                  .then_inc(y_ready, 1)

            nc.vector.memset(w_raw[:, :, :], 0.0).then_inc(dve_consts, 1)
            dve.wait_ge(ids_in, 16)
            nc.vector.tensor_copy(ids_f[:, :, :], ids_i[:, :, :]).then_inc(ids_f_ready, 1)
            for et in (et_hi, et_lo):
                nc.vector.memset(f32(et[:, :, :]).rearrange("p t (n f) -> p (t n) f", f=QUAD)[:, :, FEATURES:], 0.0)
            nc.vector.memset(ones_row[:, :], 1.0).then_inc(dve_consts, 1)
            nc.vector.memset(g_raw[:, 0:KT - 1, :], 0.0).then_inc(dve_consts, 1)
            def kept():
                dve.wait_ge(gram_ready, 2)
                dve.wait_ge(oh_copied, NOH)
                for f0, n, i0 in KEPT_RUNS:
                    last = nc.vector.tensor_copy(et_cols(et_lo, TILES - 1, f0, n), f32(keep_lo[:, i0:i0 + n, :]))
                last.then_inc(kept_lo_back, 1)

            steps = {"table": table, "group": group, "weights": weights, "gram": gram, "mlp2": mlp2, "kept": kept}
            for kind, *at in order:
                if kind in steps:
                    steps[kind](*at)


def kernel(**inputs):
    import numpy as _np
    import concourse.bacc as _bacc
    from concourse import mybir as _mybir
    from concourse.bass_utils import run_bass_kernel_spmd as _run

    nc = _bacc.Bacc("TRN2", target_bir_lowering=False, num_devices=1)
    arrays, aps = {}, {}
    for name, value in inputs.items():
        a = _np.ascontiguousarray(value)
        arrays[f"in_{name}"] = a
        aps[name] = nc.dram_tensor(f"in_{name}", a.shape, _mybir.dt.from_np(a.dtype), kind="ExternalInput").ap()
    out = nc.dram_tensor("out_y", (BATCH, 1), _mybir.dt.float32, kind="ExternalOutput").ap()
    build(nc, aps["r_dense_features"], aps["ids"], [aps[f"tbl_{s}"] for s in range(TABLES)],
          aps["W_top1"], aps["b_top1"], aps["W_top2"], aps["b_top2"], aps["W_top3"], out)
    return _run(nc, [arrays], core_ids=[0]).results[0]["out_y"]
```

```python
import concourse.bass as bass
from concourse import mybir
from contextlib import ExitStack

P = 128
BATCH = 512
TILES = BATCH // P
DIM = 128
TABLES = 26
FEATURES = TABLES + 1
H1, H2 = 512, 256
ROWS = [12500, 1000, 12500, 125000, 12500, 12500, 12500, 1000, 12500, 1250, 1000, 12500, 12500,
        1000, 1000, 1000, 1250, 1000, 1250, 12500, 1000, 1000, 1250, 1000, 1000, 1000]

ONEHOT = [15, 20, 21, 22, 23, 24, 25]
OH_PARTS = 125
KEPT_RUNS = [(16, 1, 0), (21, 6, 1)]
MAX_CHUNKS = 10
PIECE = MAX_CHUNKS // 2
RAW_SLOTS = 3
PIECE_SLOTS = 2
PAIR_LOADS_PER_PIECE = 4
OH_SLOTS = 4

GROUPS = [[17, 18, 19, 20], [12, 13, 14, 15], [8, 9, 10, 11], [4, 5, 6, 7], [0, 1, 2, 3]]
GPT = len(GROUPS)
GATHER_SLOTS = 3

SPG = 4
QUAD = 32
MOVING = FEATURES + 1
QUARTERS = 4
QG = P // SPG // QUARTERS
QCOLS = P // QUARTERS
GSTRIDE = 128
KT = (FEATURES + 3) // 4
ET_SLOTS = TILES - 1
NK = [min(KT, FEATURES - KT * q) for q in range(4)]
BIAS_ROW = 3 * QUAD + FEATURES
DENSE2 = DIM + FEATURES * TABLES // 2


def chunks(i):
    return ROWS[ONEHOT[i]] // OH_PARTS


def pair_row(g):
    return DIM + g * TABLES - g * (g - 1) // 2


def build(nc, dense, ids, tables, w1, b1, w2, b2, w3, out):
    fp32, f32r, i32 = mybir.dt.float32, mybir.dt.float32r, mybir.dt.int32
    ALU, ACT = mybir.AluOpType, mybir.ActivationFunctionType
    NOH = len(ONEHOT)
    PIECES = 2 * NOH
    NGROUPS = GPT * TILES
    first_chunk = [sum(chunks(j) for j in range(i)) for i in range(NOH + 1)]

    ctx = ExitStack()
    with ctx:
        def sb(name, shape, dt=fp32):
            return ctx.enter_context(nc.sbuf_tensor(name, shape, dt))

        def ps(name, shape, dt=fp32):
            return ctx.enter_context(nc.psum_tensor(name, shape, dt))

        def sem(name):
            return ctx.enter_context(nc.semaphore(name))

        ident = sb("ident", [P, P])
        ids_i = sb("ids_i", [P, TILES, TABLES], i32)
        ids_f = sb("ids_f", [P, TILES, TABLES])
        ids_bc = sb("ids_bc", [P, 2, BATCH], mybir.dt.float16)
        rowid = {c: sb(f"rowid{c}", [P, c]) for c in sorted({chunks(i) for i in range(NOH)})}
        dense_sb = sb("dense_sb", [P, TILES, DIM])
        gathered = sb("gathered", [P, GATHER_SLOTS, 4, DIM])
        et_hi = sb("et_hi", [P, ET_SLOTS, P * QUAD], f32r)
        et_lo = sb("et_lo", [P, ET_SLOTS, P * MOVING], f32r)
        keep_hi = sb("keep_hi", [P, NOH, P], f32r)
        keep_lo = sb("keep_lo", [P, NOH, P], f32r)
        tab_raw = sb("tab_raw", [P, RAW_SLOTS, PIECE * DIM])
        tab_hi = sb("tab_hi", [P, PIECE_SLOTS, PIECE * DIM], f32r)
        tab_lo = sb("tab_lo", [P, PIECE_SLOTS, PIECE * DIM], f32r)
        onehot = sb("onehot", [P, OH_SLOTS, BATCH], f32r)
        dense_hi = sb("dense_hi", [P, 2, P], f32r)
        dense_lo = sb("dense_lo", [P, 2, P], f32r)
        w_raw = sb("w_raw", [P, KT, H1])
        w_mask = sb("w_mask", [P, KT])
        w1_hi = sb("w1_hi", [P, KT + 1, H1], f32r)
        w1_lo = sb("w1_lo", [P, KT + 1, H1], f32r)
        w2_hi = sb("w2_hi", [P, H1 // P, H2], f32r)
        w2_lo = sb("w2_lo", [P, H1 // P, H2], f32r)
        w3_bc = sb("w3_bc", [P, H2])
        g_raw = sb("g_raw", [P, 2, KT, QCOLS])
        g_hi = sb("g_hi", [P, KT, P], f32r)
        g_lo = sb("g_lo", [P, KT, P], f32r)
        h1_sb = sb("h1_sb", [P, H1])
        h1t_hi = sb("h1t_hi", [P, H1 // P, P], f32r)
        h1t_lo = sb("h1t_lo", [P, H1 // P, P], f32r)
        y = sb("y", [P, TILES])

        gram_ps = ps("gram_ps", [P, 4 * 512])
        trans_ps = ps("trans_ps", [P, 2, 512])
        mlp_ps = ps("mlp_ps", [P, H1])
        misc_ps = ps("misc_ps", [P, 512])

        ids_in = sem("ids_in")
        dense_in = sem("dense_in")
        tab_in = [sem(f"tab_in{s}") for s in range(RAW_SLOTS)]
        above_in = sem("above_in")
        below_in = sem("below_in")
        w1_dense_in = sem("w1_dense_in")
        w2_in = sem("w2_in")
        small_in = sem("small_in")
        gather_in = [sem(f"gather_in{s}") for s in range(GATHER_SLOTS)]
        ident_zero = sem("ident_zero")
        pool_consts = sem("pool_consts")
        dve_consts = sem("dve_consts")
        ids_f_ready = sem("ids_f_ready")
        ids_ps_ready = sem("ids_ps_ready")
        ids_bc_ready = sem("ids_bc_ready")
        tab_hi_ready = sem("tab_hi_ready")
        tab_lo_ready = sem("tab_lo_ready")
        onehot_ready = sem("onehot_ready")
        chunk_done = sem("chunk_done")
        oh_done = sem("oh_done")
        oh_copied = sem("oh_copied")
        kept_hi_back = sem("kept_hi_back")
        kept_lo_back = sem("kept_lo_back")
        w_sum_ready = sem("w_sum_ready")
        w_hi_ready = sem("w_hi_ready")
        w_lo_ready = sem("w_lo_ready")
        trans_ready = sem("trans_ready")
        trans_hi_done = sem("trans_hi_done")
        trans_lo_done = sem("trans_lo_done")
        gram_ready = sem("gram_ready")
        moved_act = sem("moved_act")
        moved_dve = sem("moved_dve")
        g_hi_ready = sem("g_hi_ready")
        g_lo_ready = sem("g_lo_ready")
        h1_ready = sem("h1_ready")
        h1_relu = sem("h1_relu")
        h1t_ready = sem("h1t_ready")
        h1t_hi_ready = sem("h1t_hi_ready")
        h1t_lo_ready = sem("h1t_lo_ready")
        h2_ready = sem("h2_ready")
        y_ready = sem("y_ready")
        y_out = sem("y_out")

        def f32(ap):
            return ap.bitcast(fp32)

        def et_cols(et, t, f0, n):
            return et[:, t % ET_SLOTS, :].rearrange("p (n f) -> p f n", n=P)[:, f0:f0 + n, :]

        def et_feature(et, f):
            return et[:, :, :].rearrange("p t (n f) -> p t n f", n=P)[:, :, :, f]

        def et_stationary(t, j):
            return et_hi[:, t % ET_SLOTS, j * P:(j + 1) * P]

        def gram_block(s, q, nk, u):
            v = gram_ps[QUAD * s:QUAD * s + FEATURES, (u % 2) * QG * GSTRIDE:(u % 2 + 1) * QG * GSTRIDE]
            v = v.rearrange("p (j c) -> p c j", c=GSTRIDE)
            c0 = s * MOVING + KT * q
            return v[:, c0:c0 + nk, :]

        def g_block(s, q, nk, u):
            v = g_raw[QUAD * q:QUAD * q + FEATURES, u % 2, 0:nk, :].rearrange("p k (j s) -> p k s j", s=SPG)
            return v[:, :, s, :]

        def quarter(g, u):
            return g[:, :, u * QCOLS:(u + 1) * QCOLS]

        w1_dense_a = h1_sb[:, :]
        w1_dense_b = tab_raw[:, RAW_SLOTS - 1, 0:H1]
        b2_row = tab_raw[0:1, 0, 0:H2]
        ones_row = tab_raw[0:1, 1, 0:P]

        above_loads, below_loads = [], []
        for f in range(FEATURES - 1):
            q, k = divmod(f + 1, KT)
            r = pair_row(f) - k
            above_loads.append((w_raw[QUAD * q + f::QUAD, :, :],
                                w1[r:r + (4 - q) * KT, :].rearrange("(a k) n -> a k n", k=KT)))
        for g in range(FEATURES - 1):
            q, k = divmod(g, KT)
            below_loads.append((w_raw[QUAD * q + g + 1:QUAD * q + FEATURES, k, :],
                                w1[pair_row(g):pair_row(g) + FEATURES - 1 - g, :]))
        below_loads.append((w_raw[BIAS_ROW:BIAS_ROW + 1, KT - 1, :], b1.rearrange("(a n) -> a n", a=1)))
        STAGES = ["dense"] + list(range(KT)) + ["w2"]
        w2_raw = w_raw[:, 0:2, :].rearrange("p a n -> p (a n)").rearrange("p (c n) -> p c n", n=H2)

        block = ctx.enter_context(nc.Block())

        @block.sync
        def _(sp):
            sp.dma_start(ids_i[:, :, :], ids.rearrange("(p t) s -> p t s", t=TILES)).then_inc(ids_in, 16)

            def load_piece(n):
                i, h = n // 2, n % 2
                c = chunks(i) // 2
                if n >= RAW_SLOTS:
                    sp.wait_ge(tab_lo_ready, n - RAW_SLOTS + 1)
                src = tables[ONEHOT[i]].rearrange("(p c) d -> p (c d)", p=OH_PARTS)
                src = src[:, h * c * DIM:(h + 1) * c * DIM]
                sp.dma_start(tab_raw[0:OH_PARTS, n % RAW_SLOTS, 0:c * DIM], src).then_inc(tab_in[n % RAW_SLOTS], 16)

            load_piece(0)
            sp.dma_start(w1_dense_a, w1[0:DIM, :]).then_inc(w1_dense_in, 16)
            sp.dma_start(w1_dense_b, w1[DENSE2:DENSE2 + DIM, :]).then_inc(w1_dense_in, 16)
            load_piece(1)
            sp.dma_start(dense_sb[:, :, :], dense.rearrange("(p t) d -> p t d", t=TILES)).then_inc(dense_in, 16)
            sp.dma_start(w3_bc[:, :], w3.rearrange("a b -> (a b)").partition_broadcast(P)).then_inc(small_in, 16)
            sp.wait_ge(w_sum_ready, 1)
            load_piece(2)
            sp.wait_ge(dve_consts, 1)

            def load_pairs(a, b):
                for n in range(a, min(b, len(above_loads) + len(below_loads))):
                    if n < len(above_loads):
                        sp.dma_start(*above_loads[n]).then_inc(above_in, 16)
                    else:
                        if n == len(above_loads):
                            sp.wait_ge(above_in, 16 * n)
                        sp.dma_start(*below_loads[n - len(above_loads)]).then_inc(below_in, 16)

            for n in range(RAW_SLOTS, PIECES):
                a = (n - RAW_SLOTS) * PAIR_LOADS_PER_PIECE
                load_pairs(a, a + PAIR_LOADS_PER_PIECE)
                load_piece(n)
            load_pairs(a + PAIR_LOADS_PER_PIECE, len(above_loads) + len(below_loads))
            sp.wait_ge(tab_lo_ready, PIECES)
            sp.dma_start(b2_row, b2.rearrange("(a n) -> a n", a=1)).then_inc(small_in, 16)
            sp.wait_ge(w_lo_ready, STAGES.index(1) + 1)
            sp.dma_start(w2_raw, w2.rearrange("(c p) n -> p c n", p=P)).then_inc(w2_in, 16)
            sp.wait_ge(y_ready, TILES)
            sp.dma_start(out.rearrange("(p t) a -> p (t a)", t=TILES), y[:, :]).then_inc(y_out, 16)
            sp.wait_ge(y_out, 16)

        @block.gpsimd
        def _(pool):
            pool.memset(ident[:, :], 0.0).then_inc(ident_zero, 1)
            pool.memset(g_raw[:, :, KT - 1, :], 0.0).then_inc(ident_zero, 1)
            for c, r in rowid.items():
                pool.iota(r[:, :], pattern=[[1, c]], base=0, channel_multiplier=c,
                          allow_small_or_imprecise_dtypes=True).then_inc(pool_consts, 1)
            pool.memset(w_mask[:, :], 2.0).then_inc(ident_zero, 1)
            pool.wait_ge(ident_zero, 3)
            pool.affine_select(out=ident[:, :], in_=ident[:, :], compare_op=ALU.not_equal, fill=1.0, base=0,
                               pattern=[[-1, P]], channel_multiplier=1).then_inc(pool_consts, 1)
            pool.affine_select(out=g_raw[:, :, KT - 1, :], in_=g_raw[:, :, KT - 1, :], compare_op=ALU.not_equal,
                               fill=0.5, base=-BIAS_ROW, pattern=[[0, 2], [0, QCOLS]], channel_multiplier=1)\
                .then_inc(pool_consts, 1)
            for q in range(4):
                m = w_mask[:, 0:NK[q]]
                if q > 0:
                    pool.wait_ge(pool_consts, len(rowid) + 2 + q)
                pool.affine_select(out=m, in_=m, compare_op=ALU.not_equal, fill=0.0, base=-(QUAD + KT) * q,
                                   pattern=[[-1, NK[q]]], channel_multiplier=1).then_inc(pool_consts, 1)
            pool.wait_ge(ids_in, 16)
            for n in range(NGROUPS):
                t, fs = n // GPT, GROUPS[n % GPT]
                if n >= GATHER_SLOTS:
                    pool.wait_ge(trans_ready, n - GATHER_SLOTS + 1)
                for f in fs:
                    if f > 0:
                        pool.indirect_dma_start(
                            out=gathered[:, n % GATHER_SLOTS, f - fs[0], :], out_offset=None, in_=tables[f - 1],
                            in_offset=bass.IndirectOffsetOnAxis(ap=ids_i[:, t, f - 1:f], axis=0),
                        ).then_inc(gather_in[n % GATHER_SLOTS], 16)

        CONSTS = len(rowid) + 2 + 4

        gather_need, gather_count = [], [0] * GATHER_SLOTS
        for n in range(NGROUPS):
            gather_count[n % GATHER_SLOTS] += 16 * sum(f > 0 for f in GROUPS[n % GPT])
            gather_need.append(gather_count[n % GATHER_SLOTS])

        order = [("weights", "dense")]
        n, clock = 0, 9.0
        for piece in range(2 * NOH):
            if piece % 2 == 0 and piece // 2 + 1 < NOH:
                order.append(("ids", piece // 2 + 1))
            order.append(("piece", piece))
            clock += 2.2
            if clock > 4 + 4.2 * (n + 1):
                order.append(("group", n))
                n, clock = n + 1, clock + 0.6
            if piece >= 2 * NOH - 2:
                a = 4 * (piece - 2 * NOH + 2)
                order += [("weights", k) for k in range(a, min(a + 4, KT))]

        def groups(upto):
            nonlocal n
            order.extend(("group", m) for m in range(n, upto))
            n = max(n, upto)

        def grams(t, *us):
            order.extend(("gram", t, u) for u in us)

        groups(8)
        grams(0, 0, 1)
        groups(9)
        grams(0, 2, 3)
        order += [("weights", "w2"), ("kept",)]
        groups(10)
        order += [("mlp1", 0)]
        grams(1, 0)
        order += [("h1t", 0)]
        grams(1, 1, 2, 3)
        groups(12)
        order += [("mlp2", 0), ("mlp1", 1), ("group", 12), ("h1t", 1), ("group", 13), ("mlp2", 1), ("group", 14)]
        n = 15
        grams(2, 0, 1, 2, 3)
        groups(16)
        order += [("mlp1", 2)]
        groups(17)
        order += [("h1t", 2)]
        groups(18)
        order += [("mlp2", 2)]
        groups(20)
        grams(3, 0, 1, 2, 3)
        order += [("mlp1", 3), ("h1t", 3), ("mlp2", 3)]

        @block.tensor
        def _(pe):
            def broadcast_ids(i):
                if i == 0:
                    pe.wait_ge(ids_f_ready, 1)
                    pe.wait_ge(pool_consts, CONSTS)
                else:
                    pe.wait_ge(ids_bc_ready, i)
                for t in range(TILES):
                    s = ONEHOT[i]
                    last = nc.tensor.transpose(misc_ps[:, t * P:(t + 1) * P],
                                               ids_f[:, t, s:s + 1].broadcast_to([P, P]), ident[:, :])
                last.then_inc(ids_ps_ready, 1)

            def piece(n):
                i, h = n // 2, n % 2
                C = chunks(i)
                bank = (i % 2) * 1024
                if h == 0 and i >= 2:
                    pe.wait_ge(oh_copied, i - 1)
                pe.wait_ge(tab_lo_ready, n + 1)
                for c in range(h * C // 2, (h + 1) * C // 2):
                    x = first_chunk[i] + c
                    pe.wait_ge(onehot_ready, x + 1)
                    cc = c - h * C // 2
                    for part, src in enumerate((tab_hi, tab_lo)):
                        last = nc.tensor.matmul(gram_ps[:, bank + part * 512:bank + (part + 1) * 512],
                                                src[0:OH_PARTS, n % PIECE_SLOTS, cc * DIM:(cc + 1) * DIM],
                                                onehot[0:OH_PARTS, x % OH_SLOTS, :],
                                                start=(c == 0), stop=(c == C - 1))
                    last.then_inc(chunk_done, 1)

            def group(n):
                t, fs = n // GPT, GROUPS[n % GPT]
                if n == 0:
                    pe.wait_ge(dense_in, 16)
                if n >= 2:
                    pe.wait_ge(trans_lo_done, n - 1)
                pe.wait_ge(gather_in[n % GATHER_SLOTS], gather_need[n])
                for a, f in enumerate(fs):
                    src = gathered[:, n % GATHER_SLOTS, a, :] if f > 0 else dense_sb[:, t, :]
                    last = nc.tensor.transpose(trans_ps[:, n % 2, a * P:(a + 1) * P], src, ident[:, :])
                last.then_inc(trans_ready, 1)

            def gram(t, u):
                if (t, u) == (0, 0):
                    pe.wait_ge(oh_copied, NOH)
                    pe.wait_ge(dve_consts, 2)
                elif QUARTERS * t + u >= 2:
                    pe.wait_ge(moved_act, QUARTERS * t + u - 1)
                    pe.wait_ge(moved_dve, QUARTERS * t + u - 1)
                if u == 0:
                    pe.wait_ge(trans_lo_done, GPT * (t + 1))
                if t == TILES - 1 and u == 0:
                    pe.wait_ge(kept_hi_back, 1)
                    pe.wait_ge(kept_lo_back, 1)
                for jj in range(QG):
                    j = u * QG + jj
                    a = (u % 2) * QG * GSTRIDE + jj * GSTRIDE
                    dst = gram_ps[:, a:a + SPG * MOVING]
                    his = et_stationary(t, j).rearrange("p (s f) -> p s f", f=QUAD)[:, :, 0:MOVING]
                    los = et_lo[:, t % ET_SLOTS, j * SPG * MOVING:(j + 1) * SPG * MOVING]
                    nc.tensor.matmul(dst.rearrange("p (s f) -> p s f", f=MOVING), et_stationary(t, j), his,
                                     start=True, stop=False)
                    last = nc.tensor.matmul(dst, et_stationary(t, j), los, start=False, stop=True)
                last.then_inc(gram_ready, 1)

            def mlp1(t):
                if t == 0:
                    pe.wait_ge(w_lo_ready, KT + 1)
                else:
                    pe.wait_ge(y_ready, t)
                parts = [(dense_hi[:, t % 2, :], dense_lo[:, t % 2, :], KT)]
                parts += [(g_hi[:, k, :], g_lo[:, k, :], k) for k in range(KT)]
                for n, (hi, lo, k) in enumerate(parts):
                    if n == 1:
                        pe.wait_ge(g_lo_ready, QUARTERS * (t + 1))
                    nc.tensor.matmul(mlp_ps[:, :], hi, w1_hi[:, k, :], start=(n == 0), stop=False)
                    nc.tensor.matmul(mlp_ps[:, :], hi, w1_lo[:, k, :], start=False, stop=False)
                    last = nc.tensor.matmul(mlp_ps[:, :], lo, w1_hi[:, k, :], start=False, stop=(n == KT))
                last.then_inc(h1_ready, 1)

            def h1t(t):
                if t == 0:
                    pe.wait_ge(ids_bc_ready, NOH)
                else:
                    pe.wait_ge(h1t_lo_ready, t)
                pe.wait_ge(h1_relu, t + 1)
                for c in range(H1 // P):
                    last = nc.tensor.transpose(misc_ps[:, c * P:(c + 1) * P], h1_sb[:, c * P:(c + 1) * P], ident[:, :])
                last.then_inc(h1t_ready, 1)

            def mlp2(t):
                if t == 0:
                    pe.wait_ge(small_in, 32)
                    pe.wait_ge(dve_consts, 4)
                    pe.wait_ge(w_lo_ready, len(STAGES))
                h2_ps = mlp_ps[:, 0:H2]
                nc.tensor.matmul(h2_ps, ones_row, b2_row, start=True, stop=False)
                pe.wait_ge(h1t_lo_ready, t + 1)
                for c in range(H1 // P):
                    nc.tensor.matmul(h2_ps, h1t_hi[:, c, :], w2_hi[:, c, :], start=False, stop=False)
                    nc.tensor.matmul(h2_ps, h1t_hi[:, c, :], w2_lo[:, c, :], start=False, stop=False)
                    last = nc.tensor.matmul(h2_ps, h1t_lo[:, c, :], w2_hi[:, c, :], start=False,
                                            stop=(c == H1 // P - 1))
                last.then_inc(h2_ready, 1)

            steps = {"ids": broadcast_ids, "piece": piece, "group": group, "gram": gram, "mlp1": mlp1,
                     "h1t": h1t, "mlp2": mlp2}
            broadcast_ids(0)
            for kind, *at in order:
                if kind in steps:
                    steps[kind](*at)

        @block.scalar
        def _(act):
            def broadcast_ids(i):
                act.wait_ge(ids_ps_ready, i + 1)
                if i >= 2:
                    act.wait_ge(onehot_ready, first_chunk[i - 1])
                nc.scalar.activation(ids_bc[:, i % 2, :], misc_ps[:, :], ACT.Copy).then_inc(ids_bc_ready, 1)

            def split_piece(n):
                c = chunks(n // 2) // 2
                act.wait_ge(tab_in[n % RAW_SLOTS], 16 * (n // RAW_SLOTS + 1))
                if n >= PIECE_SLOTS:
                    m = n - PIECE_SLOTS
                    act.wait_ge(chunk_done, first_chunk[m // 2] + (m % 2 + 1) * chunks(m // 2) // 2)
                nc.scalar.activation(tab_hi[0:OH_PARTS, n % PIECE_SLOTS, 0:c * DIM],
                                     tab_raw[0:OH_PARTS, n % RAW_SLOTS, 0:c * DIM], ACT.Copy)\
                  .then_inc(tab_hi_ready, 1)

            def copy_onehot(i):
                f = ONEHOT[i] + 1
                act.wait_ge(chunk_done, first_chunk[i + 1])
                for n, (et, keep, scale) in enumerate(((et_hi, keep_hi, 0.5), (et_lo, keep_lo, 1.0))):
                    bank = gram_ps[:, (i % 2) * 1024 + n * 512:(i % 2) * 1024 + (n + 1) * 512]
                    nc.scalar.activation(et_feature(et, f),
                                         bank[:, 0:ET_SLOTS * P].rearrange("p (t n) -> p t n", n=P), ACT.Copy,
                                         scale=scale)
                    last = nc.scalar.activation(keep[:, i, :], bank[:, ET_SLOTS * P:], ACT.Copy, scale=scale)
                last.then_inc(oh_copied, 1)

            def piece(n):
                if n + 1 < PIECES:
                    split_piece(n + 1)
                if n % 2 == 1:
                    copy_onehot(n // 2)

            def group(n):
                t, fs = n // GPT, GROUPS[n % GPT]
                act.wait_ge(trans_ready, n + 1)
                if fs[0] == 0:
                    if t >= 2:
                        act.wait_ge(h1_ready, t - 1)
                    nc.scalar.activation(dense_hi[:, t % 2, :], trans_ps[:, n % 2, 0:P], ACT.Copy)
                nc.scalar.activation(et_cols(et_hi, t, fs[0], len(fs)),
                                     trans_ps[:, n % 2, 0:len(fs) * P].rearrange("p (f n) -> p f n", n=P), ACT.Copy,
                                     scale=0.5).then_inc(trans_hi_done, 1)

            def weights(w):
                if w == "dense":
                    act.wait_ge(w_sum_ready, 1)
                    src, dst, scale = w1_dense_a, w1_hi[:, KT, :], 1.0
                elif w == "w2":
                    act.wait_ge(w2_in, 16)
                    src, dst, scale = w2_raw, w2_hi[:, :, :], 1.0
                else:
                    act.wait_ge(pool_consts, CONSTS)
                    act.wait_ge(below_in, 16 * len(below_loads))
                    src, dst, scale = w_raw[:, w, :], w1_hi[:, w, :], w_mask[:, w:w + 1]
                nc.scalar.activation(dst, src, ACT.Copy, scale=scale).then_inc(w_hi_ready, 1)

            def gram(t, u):
                x = QUARTERS * t + u
                act.wait_ge(gram_ready, x + 1)
                if x == 0:
                    act.wait_ge(dve_consts, 3)
                elif x >= 2:
                    act.wait_ge(g_lo_ready, x - 1)
                for s in (0, 1):
                    for q in range(4):
                        last = nc.scalar.activation(g_block(s, q, NK[q], u), gram_block(s, q, NK[q], u), ACT.Copy)
                last.then_inc(moved_act, 1)
                if x == 0:
                    act.wait_ge(pool_consts, CONSTS)
                if u == 0 and t > 0:
                    act.wait_ge(h1_ready, t)
                act.wait_ge(moved_act, x + 1)
                act.wait_ge(moved_dve, x + 1)
                nc.scalar.activation(quarter(g_hi, u), g_raw[:, u % 2, :, :], ACT.Copy).then_inc(g_hi_ready, 1)

            def mlp1(t):
                if t == 0:
                    act.wait_ge(w_lo_ready, 1)
                else:
                    act.wait_ge(h1t_ready, t)
                act.wait_ge(h1_ready, t + 1)
                nc.scalar.activation(h1_sb[:, :], mlp_ps[:, :], ACT.Relu).then_inc(h1_relu, 1)

            def h1t(t):
                act.wait_ge(h1t_ready, t + 1)
                if t > 0:
                    act.wait_ge(h2_ready, t)
                nc.scalar.activation(h1t_hi[:, :, :], misc_ps[:, :].rearrange("p (c n) -> p c n", n=P), ACT.Copy)\
                  .then_inc(h1t_hi_ready, 1)

            def kept():
                act.wait_ge(gram_ready, 2)
                for f0, n, i0 in KEPT_RUNS:
                    last = nc.scalar.activation(et_cols(et_hi, TILES - 1, f0, n), f32(keep_hi[:, i0:i0 + n, :]),
                                                ACT.Copy)
                last.then_inc(kept_hi_back, 1)

            steps = {"ids": broadcast_ids, "piece": piece, "group": group, "weights": weights, "gram": gram,
                     "mlp1": mlp1, "h1t": h1t, "kept": kept}
            broadcast_ids(0)
            split_piece(0)
            for kind, *at in order:
                if kind in steps:
                    steps[kind](*at)

        @block.vector
        def _(dve):
            def split_piece(n):
                c = chunks(n // 2) // 2
                dve.wait_ge(tab_hi_ready, n + 1)
                nc.vector.tensor_tensor(tab_lo[0:OH_PARTS, n % PIECE_SLOTS, 0:c * DIM],
                                        tab_raw[0:OH_PARTS, n % RAW_SLOTS, 0:c * DIM],
                                        f32(tab_hi[0:OH_PARTS, n % PIECE_SLOTS, 0:c * DIM]), ALU.subtract)\
                  .then_inc(tab_lo_ready, 1)

            def onehots(i, h):
                if h == 0:
                    dve.wait_ge(ids_bc_ready, i + 1)
                C = chunks(i)
                for c in range(h * C // 2, (h + 1) * C // 2):
                    x = first_chunk[i] + c
                    if x >= OH_SLOTS:
                        dve.wait_ge(chunk_done, x - OH_SLOTS + 1)
                    nc.vector.tensor_scalar(onehot[0:OH_PARTS, x % OH_SLOTS, :], ids_bc[0:OH_PARTS, i % 2, :],
                                            rowid[C][0:OH_PARTS, c:c + 1], None, ALU.is_equal)\
                      .then_inc(onehot_ready, 1)

            def piece(n):
                if n + 1 < PIECES:
                    split_piece(n + 1)
                    onehots((n + 1) // 2, (n + 1) % 2)

            def group(n):
                t, fs = n // GPT, GROUPS[n % GPT]
                dve.wait_ge(trans_hi_done, n + 1)
                if fs[0] == 0:
                    if t >= 2:
                        dve.wait_ge(h1_ready, t - 1)
                    nc.vector.tensor_tensor(dense_lo[:, t % 2, :], trans_ps[:, n % 2, 0:P],
                                            f32(dense_hi[:, t % 2, :]), ALU.subtract)
                nc.vector.scalar_tensor_tensor(
                    out=et_cols(et_lo, t, fs[0], len(fs)), in0=f32(et_cols(et_hi, t, fs[0], len(fs))), scalar=-2.0,
                    in1=trans_ps[:, n % 2, 0:len(fs) * P].rearrange("p (f n) -> p f n", n=P),
                    op0=ALU.mult, op1=ALU.add).then_inc(trans_lo_done, 1)

            def weights(w):
                if w == "dense":
                    dve.wait_ge(w1_dense_in, 32)
                    nc.vector.tensor_tensor(w1_dense_a, w1_dense_a, w1_dense_b, ALU.add).then_inc(w_sum_ready, 1)
                    src, hi, lo, scale = w1_dense_a, w1_hi[:, KT, :], w1_lo[:, KT, :], 1.0
                elif w == "w2":
                    src, hi, lo, scale = w2_raw, w2_hi[:, :, :], w2_lo[:, :, :], 1.0
                else:
                    src, hi, lo, scale = w_raw[:, w, :], w1_hi[:, w, :], w1_lo[:, w, :], w_mask[:, w:w + 1]
                dve.wait_ge(w_hi_ready, STAGES.index(w) + 1)
                nc.vector.scalar_tensor_tensor(out=lo, in0=src, scalar=scale, in1=f32(hi), op0=ALU.mult,
                                               op1=ALU.subtract).then_inc(w_lo_ready, 1)

            def gram(t, u):
                x = QUARTERS * t + u
                dve.wait_ge(gram_ready, x + 1)
                if x >= 2:
                    dve.wait_ge(g_hi_ready, x - 1)
                for s in (2, 3):
                    for q in range(4):
                        last = nc.vector.tensor_copy(g_block(s, q, NK[q], u), gram_block(s, q, NK[q], u))
                last.then_inc(moved_dve, 1)
                if u == 0 and t > 0:
                    dve.wait_ge(h1_ready, t)
                dve.wait_ge(moved_dve, x + 1)
                dve.wait_ge(g_hi_ready, x + 1)
                nc.vector.tensor_tensor(quarter(g_lo, u), g_raw[:, u % 2, :, :], f32(quarter(g_hi, u)), ALU.subtract)\
                  .then_inc(g_lo_ready, 1)

            def h1t(t):
                dve.wait_ge(h1t_hi_ready, t + 1)
                nc.vector.tensor_tensor(h1t_lo[:, :, :], misc_ps[:, :].rearrange("p (c n) -> p c n", n=P),
                                        f32(h1t_hi[:, :, :]), ALU.subtract).then_inc(h1t_lo_ready, 1)

            def mlp2(t):
                dve.wait_ge(h2_ready, t + 1)
                nc.vector.scalar_tensor_tensor(out=mlp_ps[:, H2:2 * H2], in0=mlp_ps[:, 0:H2], scalar=0.0,
                                               in1=w3_bc[:, :], op0=ALU.max, op1=ALU.mult, accum_out=y[:, t:t + 1])\
                  .then_inc(y_ready, 1)

            nc.vector.memset(w_raw[:, :, :], 0.0).then_inc(dve_consts, 1)
            dve.wait_ge(ids_in, 16)
            nc.vector.tensor_copy(ids_f[:, :, :], ids_i[:, :, :]).then_inc(ids_f_ready, 1)
            for et, f in ((et_hi, QUAD), (et_lo, MOVING)):
                last = nc.vector.memset(f32(et[:, :, :]).rearrange("p t (n f) -> p (t n) f", f=f)[:, :, FEATURES:], 0.0)
            last.then_inc(dve_consts, 1)
            nc.vector.memset(g_raw[:, :, 0:KT - 1, :], 0.0).then_inc(dve_consts, 1)

            def kept():
                dve.wait_ge(gram_ready, 2)
                dve.wait_ge(oh_copied, NOH)
                for f0, n, i0 in KEPT_RUNS:
                    last = nc.vector.tensor_copy(et_cols(et_lo, TILES - 1, f0, n), f32(keep_lo[:, i0:i0 + n, :]))
                last.then_inc(kept_lo_back, 1)
                nc.vector.memset(ones_row, 1.0).then_inc(dve_consts, 1)

            steps = {"piece": piece, "group": group, "weights": weights, "gram": gram, "h1t": h1t, "mlp2": mlp2,
                     "kept": kept}
            dve.wait_ge(pool_consts, CONSTS)
            split_piece(0)
            onehots(0, 0)
            for kind, *at in order:
                if kind in steps:
                    steps[kind](*at)


def kernel(**inputs):
    import numpy as _np
    import concourse.bacc as _bacc
    from concourse import mybir as _mybir
    from concourse.bass_utils import run_bass_kernel_spmd as _run

    nc = _bacc.Bacc("TRN2", target_bir_lowering=False, num_devices=1)
    arrays, aps = {}, {}
    for name, value in inputs.items():
        a = _np.ascontiguousarray(value)
        arrays[f"in_{name}"] = a
        aps[name] = nc.dram_tensor(f"in_{name}", a.shape, _mybir.dt.from_np(a.dtype), kind="ExternalInput").ap()
    out = nc.dram_tensor("out_y", (BATCH, 1), _mybir.dt.float32, kind="ExternalOutput").ap()
    build(nc, aps["r_dense_features"], aps["ids"], [aps[f"tbl_{s}"] for s in range(TABLES)],
          aps["W_top1"], aps["b_top1"], aps["W_top2"], aps["b_top2"], aps["W_top3"], out)
    return _run(nc, [arrays], core_ids=[0]).results[0]["out_y"]
```

```python
import concourse.bass as bass
from concourse import mybir
from contextlib import ExitStack

P = 128
BATCH = 512
TILES = BATCH // P
DIM = 128
TABLES = 26
FEATURES = TABLES + 1
H1, H2 = 512, 256
ROWS = [12500, 1000, 12500, 125000, 12500, 12500, 12500, 1000, 12500, 1250, 1000, 12500, 12500,
        1000, 1000, 1000, 1250, 1000, 1250, 12500, 1000, 1000, 1250, 1000, 1000, 1000]

ONEHOT = [15, 20, 21, 22, 23, 24, 25]
OH_PARTS = 125
KEPT_RUNS = [(16, 1, 0), (21, 6, 1)]
MAX_CHUNKS = 10
PIECE = MAX_CHUNKS // 2
RAW_SLOTS = 5
PIECE_SLOTS = 2
OH_SLOTS = 4
ACT_PIECES = [3, 4, 5, 7, 8, 9, 11, 13]

GROUPS = [[17, 18, 19, 20], [12, 13, 14, 15], [8, 9, 10, 11], [4, 5, 6, 7], [0, 1, 2, 3]]
GPT = len(GROUPS)
GATHER_SLOTS = 6

MLP1_PARTS = [[0, 1, 2], [3, 4, 5], [6, 7]]

SPG = 4
QUAD = 32
MOVING = FEATURES + 1
QUARTERS = 4
QG = P // SPG // QUARTERS
QCOLS = P // QUARTERS
GSTRIDE = 128
KT = (FEATURES + 3) // 4
ET_SLOTS = TILES - 1
NK = [min(KT, FEATURES - KT * q) for q in range(4)]
BIAS_ROW = 3 * QUAD + FEATURES
DENSE2 = DIM + FEATURES * TABLES // 2


def chunks(i):
    return ROWS[ONEHOT[i]] // OH_PARTS


def pair_row(g):
    return DIM + g * TABLES - g * (g - 1) // 2


def build(nc, dense, ids, tables, w1, b1, w2, b2, w3, out):
    fp32, f32r, i32 = mybir.dt.float32, mybir.dt.float32r, mybir.dt.int32
    ALU, ACT = mybir.AluOpType, mybir.ActivationFunctionType
    NOH = len(ONEHOT)
    PIECES = 2 * NOH
    NGROUPS = GPT * TILES
    first_chunk = [sum(chunks(j) for j in range(i)) for i in range(NOH + 1)]
    act_chunks = [first_chunk[n // 2] + (n % 2 + 1) * chunks(n // 2) // 2 - 1 for n in ACT_PIECES]

    def made_by(x):
        on_act = sum(a < x for a in act_chunks)
        return on_act, x - on_act

    ctx = ExitStack()
    with ctx:
        def sb(name, shape, dt=fp32):
            return ctx.enter_context(nc.sbuf_tensor(name, shape, dt))

        def ps(name, shape, dt=fp32):
            return ctx.enter_context(nc.psum_tensor(name, shape, dt))

        def sem(name):
            return ctx.enter_context(nc.semaphore(name))

        ident = sb("ident", [P, P])
        ids_i = sb("ids_i", [P, TILES, TABLES], i32)
        ids_f = sb("ids_f", [P, TILES, TABLES])
        ids_bc = sb("ids_bc", [P, 2, BATCH], mybir.dt.float16)
        row_distance = sb("row_distance", [P, BATCH], mybir.dt.float16)
        rowid = {c: sb(f"rowid{c}", [P, c]) for c in sorted({chunks(i) for i in range(NOH)})}
        dense_sb = sb("dense_sb", [P, TILES, DIM])
        gathered = sb("gathered", [P, GATHER_SLOTS, 4, DIM])
        et_hi = sb("et_hi", [P, ET_SLOTS, P * QUAD], f32r)
        et_lo = sb("et_lo", [P, ET_SLOTS, P * MOVING], f32r)
        keep_hi = sb("keep_hi", [P, NOH, P], f32r)
        keep_lo = sb("keep_lo", [P, NOH, P], f32r)
        tab_raw = sb("tab_raw", [P, RAW_SLOTS, PIECE * DIM])
        tab_hi = sb("tab_hi", [P, PIECE_SLOTS, PIECE * DIM], f32r)
        tab_lo = sb("tab_lo", [P, PIECE_SLOTS, PIECE * DIM], f32r)
        onehot = sb("onehot", [P, OH_SLOTS, BATCH], f32r)
        dense_hi = sb("dense_hi", [P, 2, P], f32r)
        dense_lo = sb("dense_lo", [P, 2, P], f32r)
        w_raw = sb("w_raw", [P, KT, H1])
        w_mask = sb("w_mask", [P, KT])
        w1_hi = sb("w1_hi", [P, KT + 1, H1], f32r)
        w1_lo = sb("w1_lo", [P, KT + 1, H1], f32r)
        w2_hi = sb("w2_hi", [P, H1 // P, H2], f32r)
        w2_lo = sb("w2_lo", [P, H1 // P, H2], f32r)
        w3_bc = sb("w3_bc", [P, H2])
        g_raw = sb("g_raw", [P, 2, KT, QCOLS])
        g_hi, g_lo = [onehot[:, :, :].rearrange("p a b -> p (a b)")[:, n * KT * P:(n + 1) * KT * P]
                      .rearrange("p (k n) -> p k n", n=P) for n in (0, 1)]
        h1_sb = sb("h1_sb", [P, H1])
        h1t_hi, h1t_lo = [tab_hi[:, n, 0:H1].rearrange("p (c n) -> p c n", n=P) for n in (0, 1)]
        y = sb("y", [P, TILES])

        gram_ps = ps("gram_ps", [P, 4 * 512])
        trans_ps = ps("trans_ps", [P, 2, 512])
        mlp_ps = ps("mlp_ps", [P, H1])
        misc_ps = ps("misc_ps", [P, 512])

        ids_in = sem("ids_in")
        dense_in = sem("dense_in")
        tab_in = [sem(f"tab_in{s}") for s in range(RAW_SLOTS)]
        above_in = sem("above_in")
        below_in = sem("below_in")
        w1_dense_in = sem("w1_dense_in")
        w2_in = sem("w2_in")
        small_in = sem("small_in")
        gather_in = [sem(f"gather_in{s}") for s in range(GATHER_SLOTS)]
        ident_zero = sem("ident_zero")
        w_raw_zero = sem("w_raw_zero")
        pool_consts = sem("pool_consts")
        dve_consts = sem("dve_consts")
        ids_f_ready = sem("ids_f_ready")
        ids_ps_ready = sem("ids_ps_ready")
        ids_bc_ready = sem("ids_bc_ready")
        tab_hi_ready = sem("tab_hi_ready")
        tab_lo_ready = sem("tab_lo_ready")
        onehot_ready = sem("onehot_ready")
        act_distance = sem("act_distance")
        act_onehot_ready = sem("act_onehot_ready")
        chunk_done = sem("chunk_done")
        oh_done = sem("oh_done")
        oh_copied = sem("oh_copied")
        kept_hi_back = sem("kept_hi_back")
        kept_lo_back = sem("kept_lo_back")
        w_sum_ready = sem("w_sum_ready")
        w_hi_ready = sem("w_hi_ready")
        w_lo_ready = sem("w_lo_ready")
        trans_ready = sem("trans_ready")
        trans_hi_done = sem("trans_hi_done")
        trans_lo_done = sem("trans_lo_done")
        gram_ready = sem("gram_ready")
        moved_act = sem("moved_act")
        moved_dve = sem("moved_dve")
        g_hi_ready = sem("g_hi_ready")
        g_lo_ready = sem("g_lo_ready")
        h1_ready = sem("h1_ready")
        h1_relu = sem("h1_relu")
        h1t_ready = sem("h1t_ready")
        h1t_hi_ready = sem("h1t_hi_ready")
        h1t_lo_ready = sem("h1t_lo_ready")
        h2_ready = sem("h2_ready")
        y_ready = sem("y_ready")
        y_out = sem("y_out")

        def f32(ap):
            return ap.bitcast(fp32)

        def et_cols(et, t, f0, n):
            return et[:, t % ET_SLOTS, :].rearrange("p (n f) -> p f n", n=P)[:, f0:f0 + n, :]

        def et_feature(et, f):
            return et[:, :, :].rearrange("p t (n f) -> p t n f", n=P)[:, :, :, f]

        def et_stationary(t, j):
            return et_hi[:, t % ET_SLOTS, j * P:(j + 1) * P]

        def gram_block(s, q, nk, u):
            v = gram_ps[QUAD * s:QUAD * s + FEATURES, (u % 2) * QG * GSTRIDE:(u % 2 + 1) * QG * GSTRIDE]
            v = v.rearrange("p (j c) -> p c j", c=GSTRIDE)
            c0 = s * MOVING + KT * q
            return v[:, c0:c0 + nk, :]

        def g_block(s, q, nk, u):
            v = g_raw[QUAD * q:QUAD * q + FEATURES, u % 2, 0:nk, :].rearrange("p k (j s) -> p k s j", s=SPG)
            return v[:, :, s, :]

        def h2_bank(t):
            return misc_ps if t < TILES - 1 else gram_ps[:, 0:H1]

        HALVES = [slice(0, H1 // 2), slice(H1 // 2, H1)]

        def h1_half(half):
            return mlp_ps[:, HALVES[0]] if half == 0 else gram_ps[:, H1:H1 + H1 // 2]

        def h1_chunks(t, half):
            n = H1 // P
            return range(n) if t < TILES - 1 else range(half * n // 2, (half + 1) * n // 2)

        def h1t_bank(t, half):
            return misc_ps if half == 0 else trans_ps[:, 0, :]

        def h1t_cols(t, half):
            c = h1_chunks(t, half)
            return slice(c[0] * P, (c[-1] + 1) * P), slice(c[0], c[-1] + 1)

        def quarter(g, u):
            return g[:, :, u * QCOLS:(u + 1) * QCOLS]

        w1_dense_a = h1_sb[:, :]
        w1_dense_b = tab_raw[:, RAW_SLOTS - 1, 0:H1]
        b2_row = tab_raw[0:1, 0, 0:H2]
        ones_row = tab_raw[0:1, 1, 0:P]

        above_loads, below_loads = [], []
        for f in range(FEATURES - 1):
            q, k = divmod(f + 1, KT)
            r = pair_row(f) - k
            above_loads.append((w_raw[QUAD * q + f::QUAD, :, :],
                                w1[r:r + (4 - q) * KT, :].rearrange("(a k) n -> a k n", k=KT)))
        for g in range(FEATURES - 1):
            q, k = divmod(g, KT)
            below_loads.append((w_raw[QUAD * q + g + 1:QUAD * q + FEATURES, k, :],
                                w1[pair_row(g):pair_row(g) + FEATURES - 1 - g, :]))
        below_loads.append((w_raw[BIAS_ROW:BIAS_ROW + 1, KT - 1, :], b1.rearrange("(a n) -> a n", a=1)))
        STAGES = ["dense"] + list(range(KT)) + ["w2"]
        w2_raw = w_raw[:, 0:2, :].rearrange("p a n -> p (a n)").rearrange("p (c n) -> p c n", n=H2)

        block = ctx.enter_context(nc.Block())

        slot_of, had_before, gather_need, users, counts = [], [], [], [None] * GATHER_SLOTS, [0] * GATHER_SLOTS
        for n in range(NGROUPS):
            rows = sum(f > 0 for f in GROUPS[n % GPT])
            slot = sum(u > 0 for u in gather_need) % GATHER_SLOTS
            slot_of.append(slot)
            had_before.append(users[slot])
            counts[slot] += 16 * rows
            gather_need.append(counts[slot] if rows else 0)
            if rows:
                users[slot] = n

        @block.sync
        def _(sp):
            sp.dma_start(ids_i[:, :, :], ids.rearrange("(p t) s -> p t s", t=TILES)).then_inc(ids_in, 16)

            def load_piece(n):
                i, h = n // 2, n % 2
                c = chunks(i) // 2
                if n >= RAW_SLOTS:
                    sp.wait_ge(tab_lo_ready, n - RAW_SLOTS + 1)
                src = tables[ONEHOT[i]].rearrange("(p c) d -> p (c d)", p=OH_PARTS)
                src = src[:, h * c * DIM:(h + 1) * c * DIM]
                sp.dma_start(tab_raw[0:OH_PARTS, n % RAW_SLOTS, 0:c * DIM], src).then_inc(tab_in[n % RAW_SLOTS], 16)

            load_piece(0)
            load_piece(1)
            load_piece(2)
            load_piece(3)
            sp.dma_start(w1_dense_a, w1[0:DIM, :]).then_inc(w1_dense_in, 16)
            sp.dma_start(w1_dense_b, w1[DENSE2:DENSE2 + DIM, :]).then_inc(w1_dense_in, 16)
            sp.dma_start(dense_sb[:, :, :], dense.rearrange("(p t) d -> p t d", t=TILES)).then_inc(dense_in, 16)

            pair_loads = len(above_loads) + len(below_loads)

            def load_pairs(a, b):
                for n in range(a, b):
                    if n < len(above_loads):
                        sp.dma_start(*above_loads[n]).then_inc(above_in, 16)
                    else:
                        if n == len(above_loads):
                            sp.wait_ge(above_in, 16 * n)
                        sp.dma_start(*below_loads[n - len(above_loads)]).then_inc(below_in, 16)

            sp.wait_ge(w_sum_ready, 1)
            sp.wait_ge(w_raw_zero, 1)
            rest = PIECES - RAW_SLOTS + 1
            for i, n in enumerate(range(RAW_SLOTS - 1, PIECES)):
                load_piece(n)
                load_pairs(i * pair_loads // rest, (i + 1) * pair_loads // rest)
            sp.dma_start(w3_bc[:, :], w3.rearrange("a b -> (a b)").partition_broadcast(P)).then_inc(small_in, 16)
            sp.wait_ge(tab_lo_ready, PIECES)
            sp.dma_start(b2_row, b2.rearrange("(a n) -> a n", a=1)).then_inc(small_in, 16)
            sp.wait_ge(w_lo_ready, STAGES.index(1) + 1)
            sp.dma_start(w2_raw, w2.rearrange("(c p) n -> p c n", p=P)).then_inc(w2_in, 16)
            sp.wait_ge(y_ready, TILES)
            sp.dma_start(out.rearrange("(p t) a -> p (t a)", t=TILES), y[:, :]).then_inc(y_out, 16)
            sp.wait_ge(y_out, 16)

        @block.gpsimd
        def _(pool):
            pool.memset(ident[:, :], 0.0).then_inc(ident_zero, 1)
            pool.memset(g_raw[:, :, KT - 1, :], 0.0).then_inc(ident_zero, 1)
            for c, r in rowid.items():
                pool.iota(r[:, :], pattern=[[1, c]], base=0, channel_multiplier=c,
                          allow_small_or_imprecise_dtypes=True).then_inc(pool_consts, 1)
            pool.memset(w_mask[:, :], 2.0).then_inc(ident_zero, 1)
            pool.wait_ge(ident_zero, 3)
            pool.affine_select(out=ident[:, :], in_=ident[:, :], compare_op=ALU.not_equal, fill=1.0, base=0,
                               pattern=[[-1, P]], channel_multiplier=1).then_inc(pool_consts, 1)
            pool.affine_select(out=g_raw[:, :, KT - 1, :], in_=g_raw[:, :, KT - 1, :], compare_op=ALU.not_equal,
                               fill=0.5, base=-BIAS_ROW, pattern=[[0, 2], [0, QCOLS]], channel_multiplier=1)\
                .then_inc(pool_consts, 1)
            for q in range(4):
                m = w_mask[:, 0:NK[q]]
                if q > 0:
                    pool.wait_ge(pool_consts, len(rowid) + 2 + q)
                pool.affine_select(out=m, in_=m, compare_op=ALU.not_equal, fill=0.0, base=-(QUAD + KT) * q,
                                   pattern=[[-1, NK[q]]], channel_multiplier=1).then_inc(pool_consts, 1)
            pool.wait_ge(ids_in, 16)
            for n in range(NGROUPS):
                t, fs = n // GPT, GROUPS[n % GPT]
                if had_before[n] is not None and gather_need[n] > 0:
                    pool.wait_ge(trans_ready, had_before[n] + 1)
                for f in fs:
                    if f > 0:
                        pool.indirect_dma_start(
                            out=gathered[:, slot_of[n], f - fs[0], :], out_offset=None, in_=tables[f - 1],
                            in_offset=bass.IndirectOffsetOnAxis(ap=ids_i[:, t, f - 1:f], axis=0),
                        ).then_inc(gather_in[slot_of[n]], 16)

        IDENT_READY = len(rowid) + 1
        CONSTS = len(rowid) + 2 + 4

        order = [
            ("warm", 0, 10), ("ids", 0), ("warm", 1, 24), ("split", 0), ("zero_w_raw",), ("ids", 1),
            ("onehots", 0), ("piece", 0), ("weights", "dense"), ("split", 1), ("onehots", 1), ("split", 2),
            ("piece", 1), ("onehots", 2), ("split", 3), ("copy", 0), ("group", 0), ("onehots", 3), ("ids", 2),
            ("onehot_act", 3), ("split", 4), ("piece", 2), ("onehots", 4), ("onehot_act", 4),
            ("split", 5), ("piece", 3), ("group", 1), ("onehot_act", 5), ("ids", 3), ("piece", 4),
            ("onehots", 5), ("group", 2), ("ids", 4), ("split", 6), ("group", 3), ("onehots", 6), ("copy", 1),
            ("copy", 2), ("split", 7), ("piece", 5), ("onehots", 7), ("onehot_act", 7), ("piece", 6),
            ("onehots", 8), ("split", 8), ("group", 4), ("piece", 7), ("onehot_act", 8), ("group", 5),
            ("onehots", 9), ("split", 9), ("onehot_act", 9), ("split", 10), ("ids", 5), ("group", 6),
            ("onehots", 10), ("onehots", 11), ("piece", 8), ("piece", 9), ("copy", 3), ("group", 7),
            ("copy", 4), ("split", 11), ("piece", 10), ("onehot_act", 11), ("split", 12), ("ids", 6),
            ("copy", 5), ("onehots", 12), ("onehots", 13), ("split", 13), ("group", 8), ("piece", 11),
            ("zeros",), ("onehot_act", 13), ("piece", 12), ("group", 9), ("weights", 0), ("copy", 6),
            ("piece", 13), ("group", 10), ("weights", 1),
            ("warm", 2, 8), ("gram", 0, 0), ("weights", 2), ("gram", 0, 1), ("gram_split", 0, 0), ("group", 11),
            ("gram_split", 0, 1), ("gram", 0, 2), ("weights", 3), ("gram", 0, 3), ("weights", 4),
            ("weights", 5), ("weights", 6), ("gram_split", 0, 2), ("gram_split", 0, 3), ("group", 12),
            ("gram", 1, 0), ("gram", 1, 1), ("group", 13), ("mlp1", 0, 0), ("weights", "w2"),
            ("gram_split", 1, 0), ("mlp1", 0, 1), ("gram_split", 1, 1), ("kept",), ("relu", 0), ("mlp1", 0, 2),
            ("gram", 1, 2), ("group", 14), ("gram", 1, 3), ("gram_split", 1, 2), ("h1t", 0),
            ("gram_split", 1, 3),
            ("gram", 2, 0), ("gram", 2, 1), ("group", 15), ("group", 16), ("gram_split", 2, 0),
            ("gram_split", 2, 1), ("mlp1", 1, 0), ("mlp1", 1, 1), ("group", 17), ("mlp1", 1, 2),
            ("gram", 2, 2), ("relu", 1), ("gram_split", 2, 2), ("group", 18), ("gram", 2, 3),
            ("gram_split", 2, 3), ("mlp2", 0), ("group", 19), ("mlp1", 2, 0), ("h1t", 1),
            ("gram", 3, 0), ("mlp2", 1), ("relu", 2), ("mlp1", 2, 1), ("mlp1", 2, 2), ("gram_split", 3, 0),
            ("gram", 3, 1), ("gram_split", 3, 1), ("h1t", 2), ("gram", 3, 2), ("gram", 3, 3),
            ("gram_split", 3, 2), ("gram_split", 3, 3), ("relu", 3, 0), ("mlp2", 2), ("mlp1", 3, 0),
            ("mlp1", 3, 1), ("relu", 3, 1), ("h1t", 3, 0), ("h1t", 3, 1), ("mlp2", 3),
        ]

        @block.tensor
        def _(pe):
            def broadcast_ids(i):
                if i == 0:
                    pe.wait_ge(ids_f_ready, 1)
                    pe.wait_ge(pool_consts, IDENT_READY)
                else:
                    pe.wait_ge(ids_bc_ready, i)
                for t in range(TILES):
                    s = ONEHOT[i]
                    last = nc.tensor.transpose(misc_ps[:, t * P:(t + 1) * P],
                                               ids_f[:, t, s:s + 1].broadcast_to([P, P]), ident[:, :])
                last.then_inc(ids_ps_ready, 1)

            def warm(a, n):
                if a == 0:
                    pe.wait_ge(pool_consts, IDENT_READY)
                elif a == 2:
                    pe.wait_ge(ids_bc_ready, NOH)
                for _ in range(n):
                    nc.tensor.transpose((misc_ps if a == 2 else gram_ps)[:, 0:P], ident[:, :], ident[:, :])

            def piece(n):
                i, h = n // 2, n % 2
                C = chunks(i)
                bank = (i % 2) * 1024
                if h == 0 and i >= 2:
                    pe.wait_ge(oh_copied, i - 1)
                pe.wait_ge(tab_lo_ready, n + 1)
                for c in range(h * C // 2, (h + 1) * C // 2):
                    x = first_chunk[i] + c
                    if x in act_chunks:
                        pe.wait_ge(act_onehot_ready, made_by(x + 1)[0])
                    else:
                        pe.wait_ge(onehot_ready, made_by(x + 1)[1])
                    cc = c - h * C // 2
                    for part, src in enumerate((tab_hi, tab_lo)):
                        last = nc.tensor.matmul(gram_ps[:, bank + part * 512:bank + (part + 1) * 512],
                                                src[0:OH_PARTS, n % PIECE_SLOTS, cc * DIM:(cc + 1) * DIM],
                                                onehot[0:OH_PARTS, x % OH_SLOTS, :],
                                                start=(c == 0), stop=(c == C - 1))
                    last.then_inc(chunk_done, 1)

            def group(n):
                t, fs = n // GPT, GROUPS[n % GPT]
                if n == 0:
                    pe.wait_ge(dense_in, 16)
                if n >= 2:
                    pe.wait_ge(trans_lo_done, n - 1)
                if gather_need[n] > 0:
                    pe.wait_ge(gather_in[slot_of[n]], gather_need[n])
                for a, f in enumerate(fs):
                    src = gathered[:, slot_of[n], a, :] if f > 0 else dense_sb[:, t, :]
                    last = nc.tensor.transpose(trans_ps[:, n % 2, a * P:(a + 1) * P], src, ident[:, :])
                last.then_inc(trans_ready, 1)

            def gram(t, u):
                if (t, u) == (0, 0):
                    pe.wait_ge(oh_copied, NOH)
                    pe.wait_ge(dve_consts, 1)
                elif QUARTERS * t + u >= 2:
                    pe.wait_ge(moved_act, QUARTERS * t + u - 1)
                    pe.wait_ge(moved_dve, QUARTERS * t + u - 1)
                if u == 0:
                    pe.wait_ge(trans_lo_done, GPT * (t + 1))
                if t == TILES - 1 and u == 0:
                    pe.wait_ge(kept_hi_back, 1)
                    pe.wait_ge(kept_lo_back, 1)
                for jj in range(QG):
                    j = u * QG + jj
                    a = (u % 2) * QG * GSTRIDE + jj * GSTRIDE
                    dst = gram_ps[:, a:a + SPG * MOVING]
                    his = et_stationary(t, j).rearrange("p (s f) -> p s f", f=QUAD)[:, :, 0:MOVING]
                    los = et_lo[:, t % ET_SLOTS, j * SPG * MOVING:(j + 1) * SPG * MOVING]
                    nc.tensor.matmul(dst.rearrange("p (s f) -> p s f", f=MOVING), et_stationary(t, j), his,
                                     start=True, stop=False)
                    last = nc.tensor.matmul(dst, et_stationary(t, j), los, start=False, stop=True)
                last.then_inc(gram_ready, 1)

            def mlp1(t, part):
                whole = t < TILES - 1
                if part == 0 and t == 0:
                    pe.wait_ge(w_lo_ready, KT + 1)
                elif part == 0:
                    pe.wait_ge(h1_relu, t)
                elif not whole:
                    pe.wait_ge(moved_act, QUARTERS * TILES)
                    pe.wait_ge(moved_dve, QUARTERS * TILES)
                tiles = [(dense_hi[:, t % 2, :], dense_lo[:, t % 2, :], KT)]
                tiles += [(g_hi[:, k, :], g_lo[:, k, :], k) for k in range(KT)]
                dst, cols = (mlp_ps[:, :], slice(0, H1)) if whole else (h1_half(part), HALVES[part])
                for n in MLP1_PARTS[part] if whole else range(KT + 1):
                    hi, lo, k = tiles[n]
                    if n == 1:
                        pe.wait_ge(g_lo_ready, QUARTERS * (t + 1))
                    nc.tensor.matmul(dst, hi, w1_hi[:, k, cols], start=(n == 0), stop=False)
                    nc.tensor.matmul(dst, hi, w1_lo[:, k, cols], start=False, stop=False)
                    last = nc.tensor.matmul(dst, lo, w1_hi[:, k, cols], start=False, stop=(n == KT))
                if not whole or part == len(MLP1_PARTS) - 1:
                    last.then_inc(h1_ready, 1)

            def h1t(t, half=0):
                if t == 0:
                    pe.wait_ge(ids_bc_ready, NOH)
                elif half == 0:
                    pe.wait_ge(y_ready, t)
                else:
                    pe.wait_ge(trans_lo_done, NGROUPS)
                pe.wait_ge(h1_relu, t + 1 + half)
                for c in h1_chunks(t, half):
                    last = nc.tensor.transpose(h1t_bank(t, half)[:, c * P:(c + 1) * P], h1_sb[:, c * P:(c + 1) * P],
                                               ident[:, :])
                last.then_inc(h1t_ready, 1)

            def mlp2(t):
                if t == 0:
                    pe.wait_ge(small_in, 32)
                    pe.wait_ge(dve_consts, 3)
                    pe.wait_ge(w_lo_ready, len(STAGES))
                h2_ps = h2_bank(t)[:, 0:H2]
                if t < TILES - 1:
                    pe.wait_ge(h1t_lo_ready, t + 1)
                else:
                    pe.wait_ge(g_lo_ready, QUARTERS * TILES)
                nc.tensor.matmul(h2_ps, ones_row, b2_row, start=True, stop=False)
                for c in range(H1 // P):
                    if c == 0:
                        pe.wait_ge(h1t_lo_ready, t + 1)
                    elif t == TILES - 1 and c == H1 // P // 2:
                        pe.wait_ge(h1t_lo_ready, t + 2)
                    nc.tensor.matmul(h2_ps, h1t_hi[:, c, :], w2_hi[:, c, :], start=False, stop=False)
                    nc.tensor.matmul(h2_ps, h1t_hi[:, c, :], w2_lo[:, c, :], start=False, stop=False)
                    last = nc.tensor.matmul(h2_ps, h1t_lo[:, c, :], w2_hi[:, c, :], start=False,
                                            stop=(c == H1 // P - 1))
                last.then_inc(h2_ready, 1)

            steps = {"ids": broadcast_ids, "piece": piece, "group": group, "gram": gram, "mlp1": mlp1, "warm": warm,
                     "h1t": h1t, "mlp2": mlp2}
            for kind, *at in order:
                if kind in steps:
                    steps[kind](*at)

        @block.scalar
        def _(act):
            def broadcast_ids(i):
                act.wait_ge(ids_ps_ready, i + 1)
                if i >= 2:
                    on_act, on_dve = made_by(first_chunk[i - 1])
                    act.wait_ge(onehot_ready, on_dve)
                    if on_act > 0:
                        act.wait_ge(act_onehot_ready, on_act)
                nc.scalar.activation(ids_bc[:, i % 2, :], misc_ps[:, :], ACT.Copy).then_inc(ids_bc_ready, 1)

            def split_piece(n):
                c = chunks(n // 2) // 2
                act.wait_ge(tab_in[n % RAW_SLOTS], 16 * (n // RAW_SLOTS + 1))
                if n >= PIECE_SLOTS:
                    m = n - PIECE_SLOTS
                    act.wait_ge(chunk_done, first_chunk[m // 2] + (m % 2 + 1) * chunks(m // 2) // 2)
                nc.scalar.activation(tab_hi[0:OH_PARTS, n % PIECE_SLOTS, 0:c * DIM],
                                     tab_raw[0:OH_PARTS, n % RAW_SLOTS, 0:c * DIM], ACT.Copy)\
                  .then_inc(tab_hi_ready, 1)

            def onehot_act(n):
                i = n // 2
                x = act_chunks[ACT_PIECES.index(n)]
                c = x - first_chunk[i]
                done = ACT_PIECES.index(n)
                act.wait_ge(ids_bc_ready, i + 1)
                if done > 0:
                    act.wait_ge(act_onehot_ready, done)
                nc.scalar.activation(row_distance[0:OH_PARTS, :], ids_bc[0:OH_PARTS, i % 2, :], ACT.Abs,
                                     scale=-1.0, bias=rowid[chunks(i)][0:OH_PARTS, c:c + 1]).then_inc(act_distance, 1)
                if x >= OH_SLOTS:
                    act.wait_ge(chunk_done, x - OH_SLOTS + 1)
                act.wait_ge(act_distance, done + 1)
                nc.scalar.activation(onehot[0:OH_PARTS, x % OH_SLOTS, :], row_distance[0:OH_PARTS, :], ACT.Relu,
                                     scale=-1.0, bias=1.0).then_inc(act_onehot_ready, 1)

            def copy_onehot(i):
                f = ONEHOT[i] + 1
                act.wait_ge(chunk_done, first_chunk[i + 1])
                for n, (et, keep, scale) in enumerate(((et_hi, keep_hi, 0.5), (et_lo, keep_lo, 1.0))):
                    bank = gram_ps[:, (i % 2) * 1024 + n * 512:(i % 2) * 1024 + (n + 1) * 512]
                    nc.scalar.activation(et_feature(et, f),
                                         bank[:, 0:ET_SLOTS * P].rearrange("p (t n) -> p t n", n=P), ACT.Copy,
                                         scale=scale)
                    last = nc.scalar.activation(keep[:, i, :], bank[:, ET_SLOTS * P:], ACT.Copy, scale=scale)
                last.then_inc(oh_copied, 1)

            def group(n):
                t, fs = n // GPT, GROUPS[n % GPT]
                act.wait_ge(trans_ready, n + 1)
                if t == TILES - 1 and n % GPT == 0:
                    act.wait_ge(gram_ready, QUARTERS)
                if fs[0] == 0:
                    if t >= 2:
                        act.wait_ge(h1_ready, t - 1)
                    nc.scalar.activation(dense_hi[:, t % 2, :], trans_ps[:, n % 2, 0:P], ACT.Copy)
                nc.scalar.activation(et_cols(et_hi, t, fs[0], len(fs)),
                                     trans_ps[:, n % 2, 0:len(fs) * P].rearrange("p (f n) -> p f n", n=P), ACT.Copy,
                                     scale=0.5).then_inc(trans_hi_done, 1)

            def weights(w):
                if w == "dense":
                    act.wait_ge(w_sum_ready, 1)
                    src, dst, scale = w1_dense_a, w1_hi[:, KT, :], 1.0
                elif w == "w2":
                    act.wait_ge(w2_in, 16)
                    src, dst, scale = w2_raw, w2_hi[:, :, :], 1.0
                else:
                    act.wait_ge(pool_consts, CONSTS)
                    act.wait_ge(below_in, 16 * len(below_loads))
                    src, dst, scale = w_raw[:, w, :], w1_hi[:, w, :], w_mask[:, w:w + 1]
                nc.scalar.activation(dst, src, ACT.Copy, scale=scale).then_inc(w_hi_ready, 1)

            def gram(t, u):
                x = QUARTERS * t + u
                act.wait_ge(gram_ready, x + 1)
                if x == 0:
                    act.wait_ge(dve_consts, 2)
                elif x >= 2:
                    act.wait_ge(g_lo_ready, x - 1)
                for s in (0, 1):
                    for q in range(4):
                        last = nc.scalar.activation(g_block(s, q, NK[q], u), gram_block(s, q, NK[q], u), ACT.Copy)
                last.then_inc(moved_act, 1)

            def gram_split(t, u):
                x = QUARTERS * t + u
                if x == 0:
                    act.wait_ge(pool_consts, CONSTS)
                if u == 0 and t > 0:
                    act.wait_ge(h1_ready, t)
                act.wait_ge(moved_act, x + 1)
                act.wait_ge(moved_dve, x + 1)
                nc.scalar.activation(quarter(g_hi, u), g_raw[:, u % 2, :, :], ACT.Copy).then_inc(g_hi_ready, 1)

            def relu(t, half=0):
                if t == 0:
                    act.wait_ge(w_lo_ready, 1)
                elif half == 0:
                    act.wait_ge(h1t_ready, t)
                act.wait_ge(h1_ready, t + 1 + half)
                src, cols = (mlp_ps[:, :], slice(0, H1)) if t < TILES - 1 else (h1_half(half), HALVES[half])
                nc.scalar.activation(h1_sb[:, cols], src, ACT.Relu).then_inc(h1_relu, 1)

            def h1t(t, half=0):
                act.wait_ge(h1t_ready, t + 1 + half)
                if t > 0 and half == 0:
                    act.wait_ge(h2_ready, t)
                cols, cs = h1t_cols(t, half)
                nc.scalar.activation(h1t_hi[:, cs, :],
                                     h1t_bank(t, half)[:, cols].rearrange("p (c n) -> p c n", n=P), ACT.Copy)\
                  .then_inc(h1t_hi_ready, 1)

            def kept():
                act.wait_ge(gram_ready, QUARTERS)
                for f0, n, i0 in KEPT_RUNS:
                    last = nc.scalar.activation(et_cols(et_hi, TILES - 1, f0, n), f32(keep_hi[:, i0:i0 + n, :]),
                                                ACT.Copy)
                last.then_inc(kept_hi_back, 1)

            def zero_w_raw():
                act.wait_ge(pool_consts, 1)
                zero_times = next(iter(rowid.values()))[:, 0:1].broadcast_to([P, KT * H1])
                nc.scalar.activation(w_raw[:, :, :].rearrange("p k n -> p (k n)"), zero_times, ACT.Copy, scale=0.0)\
                  .then_inc(w_raw_zero, 1)

            steps = {"zero_w_raw": zero_w_raw, "ids": broadcast_ids, "split": split_piece,
                     "onehot_act": onehot_act, "copy": copy_onehot, "group": group, "weights": weights,
                     "gram": gram, "gram_split": gram_split, "relu": relu, "h1t": h1t, "kept": kept}
            for kind, *at in order:
                if kind in steps:
                    steps[kind](*at)

        @block.vector
        def _(dve):
            def split_piece(n):
                c = chunks(n // 2) // 2
                dve.wait_ge(tab_hi_ready, n + 1)
                nc.vector.tensor_tensor(tab_lo[0:OH_PARTS, n % PIECE_SLOTS, 0:c * DIM],
                                        tab_raw[0:OH_PARTS, n % RAW_SLOTS, 0:c * DIM],
                                        f32(tab_hi[0:OH_PARTS, n % PIECE_SLOTS, 0:c * DIM]), ALU.subtract)\
                  .then_inc(tab_lo_ready, 1)

            def onehots(n):
                i, h = n // 2, n % 2
                if h == 0:
                    dve.wait_ge(ids_bc_ready, i + 1)
                C = chunks(i)
                for c in range(h * C // 2, (h + 1) * C // 2):
                    x = first_chunk[i] + c
                    if x in act_chunks:
                        continue
                    if x >= OH_SLOTS:
                        dve.wait_ge(chunk_done, x - OH_SLOTS + 1)
                    nc.vector.tensor_scalar(onehot[0:OH_PARTS, x % OH_SLOTS, :], ids_bc[0:OH_PARTS, i % 2, :],
                                            rowid[C][0:OH_PARTS, c:c + 1], None, ALU.is_equal)\
                      .then_inc(onehot_ready, 1)

            def group(n):
                t, fs = n // GPT, GROUPS[n % GPT]
                dve.wait_ge(trans_hi_done, n + 1)
                if t == TILES - 1 and n % GPT == 0:
                    dve.wait_ge(gram_ready, QUARTERS)
                if fs[0] == 0:
                    if t >= 2:
                        dve.wait_ge(h1_ready, t - 1)
                    nc.vector.tensor_tensor(dense_lo[:, t % 2, :], trans_ps[:, n % 2, 0:P],
                                            f32(dense_hi[:, t % 2, :]), ALU.subtract)
                nc.vector.scalar_tensor_tensor(
                    out=et_cols(et_lo, t, fs[0], len(fs)), in0=f32(et_cols(et_hi, t, fs[0], len(fs))), scalar=-2.0,
                    in1=trans_ps[:, n % 2, 0:len(fs) * P].rearrange("p (f n) -> p f n", n=P),
                    op0=ALU.mult, op1=ALU.add).then_inc(trans_lo_done, 1)

            def weights(w):
                if w == "dense":
                    dve.wait_ge(w1_dense_in, 32)
                    nc.vector.tensor_tensor(w1_dense_a, w1_dense_a, w1_dense_b, ALU.add).then_inc(w_sum_ready, 1)
                    src, hi, lo, scale = w1_dense_a, w1_hi[:, KT, :], w1_lo[:, KT, :], 1.0
                elif w == "w2":
                    src, hi, lo, scale = w2_raw, w2_hi[:, :, :], w2_lo[:, :, :], 1.0
                else:
                    src, hi, lo, scale = w_raw[:, w, :], w1_hi[:, w, :], w1_lo[:, w, :], w_mask[:, w:w + 1]
                dve.wait_ge(w_hi_ready, STAGES.index(w) + 1)
                nc.vector.scalar_tensor_tensor(out=lo, in0=src, scalar=scale, in1=f32(hi), op0=ALU.mult,
                                               op1=ALU.subtract).then_inc(w_lo_ready, 1)

            def gram(t, u):
                x = QUARTERS * t + u
                dve.wait_ge(gram_ready, x + 1)
                if x == 0:
                    dve.wait_ge(dve_consts, 2)
                elif x >= 2:
                    dve.wait_ge(g_lo_ready, x - 1)
                for s in (2, 3):
                    for q in range(4):
                        last = nc.vector.tensor_copy(g_block(s, q, NK[q], u), gram_block(s, q, NK[q], u))
                last.then_inc(moved_dve, 1)

            def gram_split(t, u):
                x = QUARTERS * t + u
                if u == 0 and t > 0:
                    dve.wait_ge(h1_ready, t)
                dve.wait_ge(moved_dve, x + 1)
                dve.wait_ge(g_hi_ready, x + 1)
                nc.vector.tensor_tensor(quarter(g_lo, u), g_raw[:, u % 2, :, :], f32(quarter(g_hi, u)), ALU.subtract)\
                  .then_inc(g_lo_ready, 1)

            def h1t(t, half=0):
                dve.wait_ge(h1t_hi_ready, t + 1 + half)
                cols, cs = h1t_cols(t, half)
                nc.vector.tensor_tensor(h1t_lo[:, cs, :],
                                        h1t_bank(t, half)[:, cols].rearrange("p (c n) -> p c n", n=P),
                                        f32(h1t_hi[:, cs, :]), ALU.subtract).then_inc(h1t_lo_ready, 1)

            def mlp2(t):
                dve.wait_ge(h2_ready, t + 1)
                nc.vector.scalar_tensor_tensor(out=h2_bank(t)[:, H2:2 * H2], in0=h2_bank(t)[:, 0:H2], scalar=0.0,
                                               in1=w3_bc[:, :], op0=ALU.max, op1=ALU.mult, accum_out=y[:, t:t + 1])\
                  .then_inc(y_ready, 1)

            def zeros():
                for et, f in ((et_hi, QUAD), (et_lo, MOVING)):
                    last = nc.vector.memset(f32(et[:, :, :]).rearrange("p t (n f) -> p (t n) f", f=f)[:, :, FEATURES:],
                                            0.0)
                last.then_inc(dve_consts, 1)
                nc.vector.memset(g_raw[:, :, 0:KT - 1, :], 0.0).then_inc(dve_consts, 1)

            def kept():
                dve.wait_ge(gram_ready, QUARTERS)
                dve.wait_ge(oh_copied, NOH)
                for f0, n, i0 in KEPT_RUNS:
                    last = nc.vector.tensor_copy(et_cols(et_lo, TILES - 1, f0, n), f32(keep_lo[:, i0:i0 + n, :]))
                last.then_inc(kept_lo_back, 1)
                nc.vector.memset(ones_row, 1.0).then_inc(dve_consts, 1)

            steps = {"split": split_piece, "onehots": onehots, "group": group, "weights": weights, "gram": gram,
                     "gram_split": gram_split, "h1t": h1t, "mlp2": mlp2, "kept": kept, "zeros": zeros}
            dve.wait_ge(ids_in, 16)
            nc.vector.tensor_copy(ids_f[:, :, :], ids_i[:, :, :]).then_inc(ids_f_ready, 1)
            dve.wait_ge(pool_consts, CONSTS)
            for kind, *at in order:
                if kind in steps:
                    steps[kind](*at)


def kernel(**inputs):
    import numpy as _np
    import concourse.bacc as _bacc
    from concourse import mybir as _mybir
    from concourse.bass_utils import run_bass_kernel_spmd as _run

    nc = _bacc.Bacc("TRN2", target_bir_lowering=False, num_devices=1)
    arrays, aps = {}, {}
    for name, value in inputs.items():
        a = _np.ascontiguousarray(value)
        arrays[f"in_{name}"] = a
        aps[name] = nc.dram_tensor(f"in_{name}", a.shape, _mybir.dt.from_np(a.dtype), kind="ExternalInput").ap()
    out = nc.dram_tensor("out_y", (BATCH, 1), _mybir.dt.float32, kind="ExternalOutput").ap()
    build(nc, aps["r_dense_features"], aps["ids"], [aps[f"tbl_{s}"] for s in range(TABLES)],
          aps["W_top1"], aps["b_top1"], aps["W_top2"], aps["b_top2"], aps["W_top3"], out)
    return _run(nc, [arrays], core_ids=[0]).results[0]["out_y"]
```
